# Optimizing a Trainium2 kernel written in Bass

```python
import numpy as np
import jax
import jax.numpy as jnp

def _softmax(x, axis=-1):
    return jax.nn.softmax(x, axis=axis)

def _gelu(x):
    return jax.nn.gelu(x, approximate=True)

def _silu(x):
    return jax.nn.silu(x)

def _sigmoid(x):
    return jax.nn.sigmoid(x)

def _layernorm(x, axis=-1, eps=1e-05):
    m = jnp.mean(x, axis=axis, keepdims=True)
    v = jnp.var(x, axis=axis, keepdims=True)
    return (x - m) / jnp.sqrt(v + eps)

def _scatter_add(tgt, idx, src, axis=0):
    return tgt.at[idx].add(src)

def _segment_sum(src, seg, n):
    return jax.ops.segment_sum(src, seg, n)
kernel_name = 'mk_prb_d1_jaxref_r8_228753'

def setup_inputs(seed: int=0):
    np.random.seed(seed)
    _w = jnp.asarray

    def _L0_attn_setup():
        import jax, jax.numpy as jnp
        import numpy as np
        DIM = 256
        H = 32
        N = 128
        G = 1
        K = 4
        HID = 512
        P = HID // H
        CHUNK = 32
        EPS = 1e-06
        DT_MIN, DT_MAX = (0.001, 0.1)

        def _causal_conv_silu(xBC, w, bias):
            b, s, c = xBC.shape
            xp = jnp.pad(xBC, ((0, 0), (K - 1, 0), (0, 0)))
            y = sum((xp[:, k:k + s, :] * w[:, k] for k in range(K))) + bias
            return jax.nn.silu(y)

        def _chunked_scan(x, dt, A, B, C, D):
            b, s, h, p = x.shape
            n = B.shape[-1]
            nc, L = (s // CHUNK, CHUNK)
            xc = x.reshape(b, nc, L, h, p)
            dtc = dt.reshape(b, nc, L, h)
            Bc = B.reshape(b, nc, L, n)
            Cc = C.reshape(b, nc, L, n)
            dA = dtc * A
            dA_cs = jnp.cumsum(dA, axis=2)
            seg = dA_cs[:, :, :, None, :] - dA_cs[:, :, None, :, :]
            mask = jnp.tril(jnp.ones((L, L), bool))[None, None, :, :, None]
            decay = jnp.exp(jnp.where(mask, seg, -jnp.inf))
            CB = jnp.einsum('bcln,bcsn->bcls', Cc, Bc)
            y_intra = jnp.einsum('bcls,bclsh,bcsh,bcshp->bclhp', CB, decay, dtc, xc)
            decay_states = jnp.exp(dA_cs[:, :, -1:, :] - dA_cs)
            states = jnp.einsum('bclh,bclh,bclhp,bcln->bchpn', decay_states, dtc, xc, Bc)
            dA_chunk = dA_cs[:, :, -1, :]

            def step(prev, inp):
                st, dec = inp
                new = prev * jnp.exp(dec)[:, :, None, None] + st
                return (new, prev)
            init = jnp.zeros((b, h, p, n), x.dtype)
            _, prev_states = jax.lax.scan(step, init, (jnp.moveaxis(states, 1, 0), jnp.moveaxis(dA_chunk, 1, 0)))
            prev_states = jnp.moveaxis(prev_states, 0, 1)
            y_inter = jnp.einsum('bcln,bclh,bchpn->bclhp', Cc, jnp.exp(dA_cs), prev_states)
            y = (y_intra + y_inter).reshape(b, s, h, p)
            return y + x * D[None, None, :, None]
        key = jax.random.key(seed)
        ks = jax.random.split(key, 8)
        b, s = (2, 256)
        d_in = 2 * HID + 2 * G * N + H
        conv_dim = HID + 2 * G * N
        return {'x': jax.random.normal(ks[0], (b, s, DIM), jnp.float32), 'W_in': jax.random.normal(ks[1], (d_in, DIM), jnp.float32) / np.sqrt(DIM), 'conv_w': jax.random.normal(ks[2], (conv_dim, K), jnp.float32) / np.sqrt(K), 'conv_b': jnp.zeros((conv_dim,), jnp.float32), 'dt_bias': jnp.zeros((H,), jnp.float32), 'A_log': jnp.log(jax.random.uniform(ks[3], (H,), jnp.float32, 1.0, 16.0)), 'D': jnp.ones((H,), jnp.float32), 'norm_w': jnp.ones((HID,), jnp.float32), 'W_out': jax.random.normal(ks[4], (DIM, HID), jnp.float32) / np.sqrt(HID)}
    _L0_attn_in = _L0_attn_setup()

    def _L0_ffn_setup():
        import jax, jax.numpy as jnp
        import numpy as np
        B, S, H, I = (1, 64, 256, 768)

        def _quantized_matmul(x, w, scale):
            wq = w.astype(jnp.float8_e4m3fn).astype(x.dtype)
            y = jnp.einsum('bsi,io->bso', x, wq)
            return y * scale
        key = jax.random.key(seed)
        ks = jax.random.split(key, 7)
        return {'x': jax.random.normal(ks[0], (B, S, H), dtype=jnp.float32), 'gate_w': jax.random.normal(ks[1], (H, I), dtype=jnp.float32) * 0.02, 'up_w': jax.random.normal(ks[2], (H, I), dtype=jnp.float32) * 0.02, 'down_w': jax.random.normal(ks[3], (I, H), dtype=jnp.float32) * 0.02, 'gate_scale': jax.random.uniform(ks[4], (I,), dtype=jnp.float32, minval=0.5, maxval=1.5), 'up_scale': jax.random.uniform(ks[5], (I,), dtype=jnp.float32, minval=0.5, maxval=1.5), 'down_scale': jax.random.uniform(ks[6], (H,), dtype=jnp.float32, minval=0.5, maxval=1.5)}
    _L0_ffn_in = _L0_ffn_setup()
    _d = {'L0_attn_x': _L0_attn_in['x'], 'L0_attn_W_in': _L0_attn_in['W_in'], 'L0_attn_conv_w': _L0_attn_in['conv_w'], 'L0_attn_conv_b': _L0_attn_in['conv_b'], 'L0_attn_dt_bias': _L0_attn_in['dt_bias'], 'L0_attn_A_log': _L0_attn_in['A_log'], 'L0_attn_D': _L0_attn_in['D'], 'L0_attn_norm_w': _L0_attn_in['norm_w'], 'L0_attn_W_out': _L0_attn_in['W_out'], 'L0_ffn_gate_w': _L0_ffn_in['gate_w'], 'L0_ffn_up_w': _L0_ffn_in['up_w'], 'L0_ffn_down_w': _L0_ffn_in['down_w'], 'L0_ffn_gate_scale': _L0_ffn_in['gate_scale'], 'L0_ffn_up_scale': _L0_ffn_in['up_scale'], 'L0_ffn_down_scale': _L0_ffn_in['down_scale']}
    _x0 = _d['L0_attn_x']
    _d['L0_attn_x'] = jax.random.normal(jax.random.fold_in(jax.random.key(seed), 1), (2, 512, 256), dtype=_x0.dtype)
    del _x0
    return _d

def reference(L0_attn_x, L0_attn_W_in, L0_attn_conv_w, L0_attn_conv_b, L0_attn_dt_bias, L0_attn_A_log, L0_attn_D, L0_attn_norm_w, L0_attn_W_out, L0_ffn_gate_w, L0_ffn_up_w, L0_ffn_down_w, L0_ffn_gate_scale, L0_ffn_up_scale, L0_ffn_down_scale):

    def _L0_attn_ref(x, W_in, conv_w, conv_b, dt_bias, A_log, D, norm_w, W_out):
        import jax, jax.numpy as jnp
        import numpy as np
        DIM = 256
        H = 32
        N = 128
        G = 1
        K = 4
        HID = 512
        P = HID // H
        CHUNK = 32
        EPS = 1e-06
        DT_MIN, DT_MAX = (0.001, 0.1)

        def _causal_conv_silu(xBC, w, bias):
            b, s, c = xBC.shape
            xp = jnp.pad(xBC, ((0, 0), (K - 1, 0), (0, 0)))
            y = sum((xp[:, k:k + s, :] * w[:, k] for k in range(K))) + bias
            return jax.nn.silu(y)

        def _chunked_scan(x, dt, A, B, C, D):
            b, s, h, p = x.shape
            n = B.shape[-1]
            nc, L = (s // CHUNK, CHUNK)
            xc = x.reshape(b, nc, L, h, p)
            dtc = dt.reshape(b, nc, L, h)
            Bc = B.reshape(b, nc, L, n)
            Cc = C.reshape(b, nc, L, n)
            dA = dtc * A
            dA_cs = jnp.cumsum(dA, axis=2)
            seg = dA_cs[:, :, :, None, :] - dA_cs[:, :, None, :, :]
            mask = jnp.tril(jnp.ones((L, L), bool))[None, None, :, :, None]
            decay = jnp.exp(jnp.where(mask, seg, -jnp.inf))
            CB = jnp.einsum('bcln,bcsn->bcls', Cc, Bc)
            y_intra = jnp.einsum('bcls,bclsh,bcsh,bcshp->bclhp', CB, decay, dtc, xc)
            decay_states = jnp.exp(dA_cs[:, :, -1:, :] - dA_cs)
            states = jnp.einsum('bclh,bclh,bclhp,bcln->bchpn', decay_states, dtc, xc, Bc)
            dA_chunk = dA_cs[:, :, -1, :]

            def step(prev, inp):
                st, dec = inp
                new = prev * jnp.exp(dec)[:, :, None, None] + st
                return (new, prev)
            init = jnp.zeros((b, h, p, n), x.dtype)
            _, prev_states = jax.lax.scan(step, init, (jnp.moveaxis(states, 1, 0), jnp.moveaxis(dA_chunk, 1, 0)))
            prev_states = jnp.moveaxis(prev_states, 0, 1)
            y_inter = jnp.einsum('bcln,bclh,bchpn->bclhp', Cc, jnp.exp(dA_cs), prev_states)
            y = (y_intra + y_inter).reshape(b, s, h, p)
            return y + x * D[None, None, :, None]
        b, s, _ = x.shape
        zxbcdt = x @ W_in.T
        z, xBC, dt = jnp.split(zxbcdt, [HID, 2 * HID + 2 * G * N], axis=-1)
        xBC = _causal_conv_silu(xBC, conv_w, conv_b)
        xs, B, C = jnp.split(xBC, [HID, HID + G * N], axis=-1)
        A = -jnp.exp(A_log)
        dt = jnp.clip(jax.nn.softplus(dt + dt_bias), DT_MIN, DT_MAX)
        xs = xs.reshape(b, s, H, P)
        y = _chunked_scan(xs, dt, A, B, C, D).reshape(b, s, HID)
        y = y * jax.nn.silu(z)
        y = y * jax.lax.rsqrt(jnp.mean(y * y, axis=-1, keepdims=True) + EPS) * norm_w
        return y @ W_out.T

    def _L0_ffn_ref(x, gate_w, up_w, down_w, gate_scale, up_scale, down_scale):
        import jax, jax.numpy as jnp
        import numpy as np
        B, S, H, I = (1, 64, 256, 768)

        def _quantized_matmul(x, w, scale):
            wq = w.astype(jnp.float8_e4m3fn).astype(x.dtype)
            y = jnp.einsum('bsi,io->bso', x, wq)
            return y * scale
        gate = jax.nn.silu(_quantized_matmul(x, gate_w, gate_scale))
        up = _quantized_matmul(x, up_w, up_scale)
        fuse = gate * up
        return _quantized_matmul(fuse, down_w, down_scale)
    x = L0_attn_x
    xn = _layernorm(x, axis=-1)
    x = x + _L0_attn_ref(xn, L0_attn_W_in, L0_attn_conv_w, L0_attn_conv_b, L0_attn_dt_bias, L0_attn_A_log, L0_attn_D, L0_attn_norm_w, L0_attn_W_out) + _L0_ffn_ref(xn, L0_ffn_gate_w, L0_ffn_up_w, L0_ffn_down_w, L0_ffn_gate_scale, L0_ffn_up_scale, L0_ffn_down_scale)
    return x

_drawn_inputs = setup_inputs


def setup_inputs(seed=0):
    import zlib

    import numpy as np

    out = dict(_drawn_inputs(seed))
    spreads = {'L0_attn_conv_b': (0.0, 0.8),
     'L0_attn_dt_bias': (0.0, 2.0),
     'L0_attn_D': (1.0, 0.6),
     'L0_attn_norm_w': (1.0, 0.6)}
    factors = {'L0_ffn_gate_scale': 7.642,
     'L0_ffn_up_scale': 8.0,
     'L0_ffn_down_scale': 8.0,
     'L0_attn_A_log': 4.207}
    for name, (base, spread) in spreads.items():
        noise = np.random.default_rng([zlib.crc32(name.encode()), seed]).standard_normal(out[name].shape)
        drawn = base * np.exp(spread * noise) if base else spread * noise
        out[name] = jnp.asarray(drawn.astype(out[name].dtype))
    for name, factor in factors.items():
        out[name] = (out[name] * factor).astype(out[name].dtype)
    return out
```

```python
from contextlib import ExitStack

import concourse.bass as bass
from concourse import mybir

ALU = mybir.AluOpType
ACT = mybir.ActivationFunctionType
F32 = mybir.dt.float32
F32R = mybir.dt.float32r
BF16 = mybir.dt.bfloat16
U32 = mybir.dt.uint32

P = 128
LC = 64
NS = 128
HP = 16
LN_EPS = 1e-5
RMS_EPS = 1e-6
DT_MIN, DT_MAX = 0.001, 0.1
EXPONENT = 0x7F800000
E4M3_MIN_NORMAL = 2.0 ** -6
ROUND_TO_E4M3 = 1.5 * 2.0 ** 20

N_PARAMS = 12
CONV_ORDER = (4, 5, 0, 1, 2, 3)

PRELUDE = [("w_a0", 0), ("w_a1", 1), ("w_b0", 2), ("w_b1", 3), ("w_c0", 4), ("w_c1", 5),
           ("wo_0", 6), ("wo_1", 7)]
BATCH = ([("xn_0", 0), ("xn_1", 1), ("dt", 2)]
         + [("conv_4", 3), ("conv_5", 4), ("conv_0", 5), ("conv_1", 6), ("conv_2", 7), ("conv_3", 0)]
         + [("dtok", 2), ("cs", 1), ("csT", 2)]
         + [(f"z_{i}", 3 + i) for i in range(4)]
         + [("cb", 7)]
         + [(f"xtok_{t}", t) for t in range(4)] + [("btok", 4)]
         + [(f"gu_{i}", (5, 6, 7, 4)[i % 4]) for i in range(12)]
         + [(f"s_{c}", c % 2) for c in range(7)] + [(f"inter_{t}", 2 + t % 2) for t in range(4)]
         + [("y_0", 0), ("y_1", 1), ("down_0", 4), ("y_2", 0), ("down_1", 5), ("y_3", 1)]
         + [("out_0", 2), ("out_1", 3), ("ssq", 6)])


def number_jobs(batches):
    last, fills, found = [None] * 8, [0] * 8, {}
    for b, name, bank in [(0, *j) for j in PRELUDE] + [(b, *j) for b in range(batches) for j in BATCH]:
        found[name, b] = bank, last[bank], fills[bank]
        last[bank] = name, b
        if not name.startswith("inter"):
            fills[bank] += 1
    return found


def mamba_and_ffn_block(nc, x, w_in, conv_w, conv_b, dt_bias, a_log, d_skip, norm_w, w_out,
                        gate_w, up_w, down_w, gate_scale, up_scale, down_scale, out):
    NB, S, DIM = x.shape
    H = a_log.shape[0]
    HID = norm_w.shape[0]
    CONV = conv_w.shape[0]
    I = gate_w.shape[1]
    TAPS = conv_w.shape[1]
    NT = S // P
    NC = S // LC
    KT = DIM // P
    NM = HID // P
    NV = CONV // P
    NI = I // P
    NG = H // 2
    GM = NG // NM
    JOB = number_jobs(NB)

    with ExitStack() as ctx:
        def sb(name, shape, dt=F32):
            return ctx.enter_context(nc.sbuf_tensor(name, shape, dt))

        def sem(name):
            return ctx.enter_context(nc.semaphore(name))

        bank = [ctx.enter_context(nc.psum_tensor(f"bank{i}", [P, 512], F32)) for i in range(8)]
        cs_dram = nc.dram_tensor("cs_scratch", [NB, H, S], F32).ap()

        ident = sb("ident", [P, P])
        tri = sb("tri", [P, P], BF16)
        suffix = sb("suffix", [P, P], BF16)
        whole = sb("whole", [P, 2, P], BF16)
        causal = sb("causal", [P, LC])
        ones = sb("ones", [P, 1])
        eps = sb("eps", [P, 2])
        convw = sb("convw", [P, NV, TAPS])
        convb = sb("convb", [P, NV])
        heads = sb("heads", [P, 4])
        dcol = sb("dcol", [P, NM])
        normw = sb("normw", [P, NM])
        gscale = sb("gscale", [P, NI])
        uscale = sb("uscale", [P, NI])
        dscale = sb("dscale", [P, DIM])
        w_hi = sb("w_hi", [P, KT, 2 * HID + 2 * NS + H], F32R)
        w_lo = sb("w_lo", [P, KT, 2 * HID + 2 * NS + H], F32R)
        woT = sb("woT", [P, NM, DIM])
        gate_q = sb("gate_q", [P, KT, I], F32R)
        up_q = sb("up_q", [P, KT, I], F32R)
        down_q = sb("down_q", [P, NI, DIM], F32R)
        x_sb = sb("x_sb", [P, NB * NT, DIM])
        stats = sb("stats", [P, NT, 6])
        meanvar = sb("meanvar", [P, NT, 2])
        std = sb("std", [P, NT])
        rstd = sb("rstd", [P, NT])
        xn = sb("xn", [P, NT, DIM])
        xn_hi = sb("xn_hi", [P, KT, S], F32R)
        xn_lo = sb("xn_lo", [P, KT, S], F32R)
        xbc = sb("xbc", [P, NV, S])
        sz = sb("sz", [P, NM, S])
        dtA = sb("dtA", [P, S])
        csT = sb("csT", [H, S])
        dtok = sb("dtok", [P, NT, H])
        rest1 = sb("rest1", [P, NT, H])
        da_hi = sb("da_hi", [P, NT, H], BF16)
        da_mid = sb("da_mid", [P, NT, H], BF16)
        da_lo = sb("da_lo", [P, NT, H], BF16)
        cs_s = sb("cs_s", [P, NG, NC])
        decay_in = sb("decay_in", [P, NT, H])
        decay_out = sb("decay_out", [P, NT, H])
        decay_all = sb("decay_all", [P, NC, H])
        cbm = sb("cbm", [P, NC, LC])
        mix = sb("mix", [P, NG, S])
        xdt = sb("xdt", [P, NC, HID])
        xw = sb("xw", [P, NT, HID])
        btok = sb("btok", [P, NC, NS])
        state = sb("state", [P, 2, HID])
        inter = sb("inter", [P, NT, HID])
        ytmp = sb("ytmp", [P, 2, S])
        sqsum = sb("sqsum", [P, S])
        fuse = sb("fuse", [P, 2, S])
        fuse_hi = sb("fuse_hi", [P, NI, S], F32R)
        fuse_lo = sb("fuse_lo", [P, NI, S], F32R)
        rms = sb("rms", [P, NT])
        rrms = sb("rrms", [P, NT])
        res = sb("res", [P, NT, DIM])

        mix_flat = mix[:, :, :].rearrange("p g t -> p (g t)")
        w_nat = mix_flat[:, 0:10 * DIM].rearrange("p (r k) -> p r k", k=DIM)
        w_dt_nat = mix_flat[:, 10 * DIM:11 * DIM]
        wo_nat = mix_flat[:, 11 * DIM:11 * DIM + 2 * HID].rearrange("p (r k) -> p r k", k=HID)
        magic = mix_flat[:, 4096:4096 + KT * I]
        down_nat = mix_flat[:, 4096 + KT * I:4096 + 2 * KT * I]
        gate_nat = inter[:, :, :].rearrange("p t c -> p (t c)")[:, 0:KT * I]
        up_nat = xw[:, :, :].rearrange("p t c -> p (t c)")[:, 0:KT * I]

        full = [sem(f"bank{i}_full") for i in range(8)]
        x_in = [sem(f"x_in{t}") for t in range(NB * NT)]
        w_a_in, w_b_in, w_c_in, w_out_in = sem("w_a_in"), sem("w_b_in"), sem("w_c_in"), sem("w_out_in")
        gate_in, up_in, down_in = sem("gate_in"), sem("up_in"), sem("down_in")
        params_in = sem("params_in")
        ident_zero, ident_ready = sem("ident_zero"), sem("ident_ready")
        masks_step, masks_ready = sem("masks_step"), sem("masks_ready")
        zeros_ready = sem("zeros_ready")
        stats_done, meanvar_done, std_ready, rstd_ready, xn_ready = (
            sem(n) for n in ("stats_done", "meanvar_done", "std_ready", "rstd_ready", "xn_ready"))
        w_hi_ready, w_lo_ready, wo_ready = sem("w_hi_ready"), sem("w_lo_ready"), sem("wo_ready")
        expo_step, magic_ready, added, ffn_q_ready = (
            sem("expo_step"), sem("magic_ready"), sem("added"), sem("ffn_q_ready"))
        xn_hi_ready, xn_lo_ready = sem("xn_hi_ready"), sem("xn_lo_ready")
        dt_exp, dt_ln, dt_clipped, da_ready = sem("dt_exp"), sem("dt_ln"), sem("dt_clipped"), sem("da_ready")
        a_exp, a_neg = sem("a_exp"), sem("a_neg")
        dtok_step, da_split = sem("dtok_step"), sem("da_split")
        csT_ready, cs_stored, decays_ready, cs_s_ready, decay_out_ready = (
            sem(n) for n in ("csT_ready", "cs_stored", "decays_ready", "cs_s_ready", "decay_out_ready"))
        cs_spread = [sem(f"cs_spread{m}") for m in range(NM)]
        sz_ready = sem("sz_ready")
        tap_done, tap_step, conv_done, silu_done = (
            sem("tap_done"), sem("tap_step"), sem("conv_done"), sem("silu_done"))
        dtok_copied, inter_zero = sem("dtok_copied"), sem("inter_zero")
        cbm_ready, xdt_ready, xw_ready, btok_ready = (
            sem("cbm_ready"), sem("xdt_ready"), sem("xw_ready"), sem("btok_ready"))
        state_scaled, state_ready, inter_done, inter_ready = (
            sem("state_scaled"), sem("state_ready"), sem("inter_done"), sem("inter_ready"))
        seg_ready, seg_capped, seg_exp, mix_ready = (
            sem("seg_ready"), sem("seg_capped"), sem("seg_exp"), sem("mix_ready"))
        gate_ready, fuse_ready, hi_ready, lo_ready = (
            sem("gate_ready"), sem("fuse_ready"), sem("hi_ready"), sem("lo_ready"))
        skip_added, y_ready, square_ready, sqsum_ready = (
            sem("skip_added"), sem("y_ready"), sem("square_ready"), sem("sqsum_ready"))
        rms_ready, rrms_ready, ffn_out, ffn_res, res_ready, stored = (
            sem(n) for n in ("rms_ready", "rrms_ready", "ffn_out", "ffn_res", "res_ready", "stored"))

        def wait_filled(eng, name, b=0):
            k, _, n = JOB[name, b]
            eng.wait_ge(full[k], n + 1)
            return bank[k]

        def bank_of(name, b=0):
            return bank[JOB[name, b][0]]

        def read_out(name, b):
            kind, _, i = name.rpartition("_")
            i = int(i) if i.isdigit() else 0
            return {
                "w": lambda: (w_lo_ready, 1 + ("a0", "a1", "b0", "b1", "c0", "c1").index(name[2:])),
                "wo": lambda: (wo_ready, 2 * i + 2),
                "xn": lambda: (xn_lo_ready, b * KT + i + 1),
                "dt": lambda: (dt_exp, b + 1),
                "conv": lambda: (conv_done, b * NV + CONV_ORDER.index(i) + 1),
                "dtok": lambda: (dtok_step, 3 * b + 2),
                "cs": lambda: (cs_s_ready, 4 * b + 4),
                "csT": lambda: (csT_ready, b + 1),
                "z": lambda: (sz_ready, b * NM + i + 1),
                "cb": lambda: (cbm_ready, b + 1),
                "xtok": lambda: (xdt_ready, 4 * (b * NT + i + 1)),
                "btok": lambda: (btok_ready, NC * (b + 1)),
                "gu": lambda: (fuse_ready if i % 2 else gate_ready, b * NI + i // 2 + 1),
                "s": lambda: (state_ready, b * (NC - 1) + i + 1),
                "inter": lambda: (inter_ready, b * NT + i + 1),
                "y": lambda: (skip_added, b * NM + i + 1),
                "down": lambda: (ffn_out, b * NT + 2 * i + 2),
                "out": lambda: (res_ready, b * NT + 2 * i + 2),
                "ssq": lambda: (rms_ready, b + 1),
            }[kind or name]()

        block = ctx.enter_context(nc.Block())

        @block.sync
        def _(sp):
            w_rows = w_in[0:10 * P, :].rearrange("(r p) k -> p r k", p=P)
            for t in range(NT):
                sp.dma_start(x_sb[:, t, :], x[0, t * P:(t + 1) * P, :]).then_inc(x_in[t], 16)
            sp.dma_start(w_nat[:, 4:8, :], w_rows[:, 4:8, :]).then_inc(w_a_in, 16)
            sp.dma_start(w_nat[:, 8:10, :], w_rows[:, 8:10, :]).then_inc(w_b_in, 16)
            sp.dma_start(w_dt_nat[0:H, :], w_in[10 * P:10 * P + H, :]).then_inc(w_b_in, 16)
            sp.dma_start(w_nat[:, 0:4, :], w_rows[:, 0:4, :]).then_inc(w_c_in, 16)
            sp.dma_start(gate_nat.rearrange("p (k i) -> p k i", i=I),
                         gate_w.rearrange("(k p) i -> p k i", p=P)).then_inc(gate_in, 16)
            sp.dma_start(wo_nat, w_out.rearrange("(r p) c -> p r c", p=P)).then_inc(w_out_in, 16)
            sp.dma_start(up_nat.rearrange("p (k i) -> p k i", i=I),
                         up_w.rearrange("(k p) i -> p k i", p=P)).then_inc(up_in, 16)
            sp.dma_start(down_nat.rearrange("p (k i) -> p k i", i=DIM),
                         down_w.rearrange("(k p) i -> p k i", p=P)).then_inc(down_in, 16)
            for t in range(NT):
                sp.dma_start(x_sb[:, NT + t, :], x[1, t * P:(t + 1) * P, :]).then_inc(x_in[NT + t], 16)

            def spread_cs(b):
                sp.wait_ge(csT_ready, b + 1)
                sp.dma_start(cs_dram[b], csT[:, :]).then_inc(cs_stored, 16)
                sp.wait_ge(cs_stored, 16 * (b + 1))
                for m in range(NM):
                    if b:
                        wait_filled(sp, f"y_{m}", b - 1)
                    elif m < 2:
                        for name in ("w_a1", "w_b1", "w_c1", "wo_1"):
                            wait_filled(sp, name)
                    else:
                        sp.wait_ge(ffn_q_ready, 3)
                    for j in range(2):
                        src = bass.AP(tensor=cs_dram.tensor, offset=(b * H + 2 * GM * m + j) * S,
                                      ap=[[0, LC], [2 * S, GM], [1, S]])
                        sp.dma_start(mix[j * LC:(j + 1) * LC, m * GM:(m + 1) * GM, :],
                                     src).then_inc(cs_spread[m], 16)

            def store(b):
                for t in range(NT):
                    sp.wait_ge(res_ready, b * NT + t + 1)
                    sp.dma_start(out[b, t * P:(t + 1) * P, :], res[:, t, :]).then_inc(stored, 16)

            for b in range(NB):
                spread_cs(b)
                store(b)
            sp.wait_ge(stored, 16 * NT * NB)

        @block.gpsimd
        def _(pool):
            n_params = 0
            with nc.allow_non_contiguous_dma(reason="small parameters"):
                for dst, src in (
                        (convw[:, :, :], conv_w.rearrange("(m p) k -> p m k", p=P)),
                        (convb[:, :], conv_b.rearrange("(m p) -> p m", p=P)),
                        (heads[3 * H:4 * H, 0:1], dt_bias.rearrange("(h o) -> h o", o=1)),
                        (heads[3 * H:4 * H, 1:2], a_log.rearrange("(h o) -> h o", o=1)),
                        (normw[:, :], norm_w.rearrange("(m p) -> p m", p=P)),
                        (gscale[:, :], gate_scale.rearrange("(m p) -> p m", p=P)),
                        (uscale[:, :], up_scale.rearrange("(m p) -> p m", p=P)),
                        (dscale[:, :], down_scale.partition_broadcast(P)),
                ) + tuple(
                        (dcol[:, m:m + 1], bass.AP(tensor=d_skip.tensor, offset=m * (P // HP),
                                                   ap=[[1, P // HP], [0, HP], [1, 1]]))
                        for m in range(NM)):
                    pool.dma_start(dst, src).then_inc(params_in, 16)
                    n_params += 1
            assert n_params == N_PARAMS

            pool.memset(ident[:, :], 0.0).then_inc(ident_zero, 1)
            pool.wait_ge(ident_zero, 1)
            pool.affine_select(out=ident[:, :], in_=ident[:, :], compare_op=ALU.not_equal, fill=1.0,
                               base=0, pattern=[[-1, P]], channel_multiplier=1).then_inc(ident_ready, 1)
            pool.memset(tri[:, :], 1.0).then_inc(masks_step, 1)
            pool.memset(suffix[:, :], 1.0).then_inc(masks_step, 1)
            pool.memset(whole[:, :, :], 0.0).then_inc(masks_step, 1)
            pool.wait_ge(masks_step, 3)
            pool.affine_select(out=tri[:, :], in_=tri[:, :], compare_op=ALU.is_ge, fill=0.0, base=0,
                               pattern=[[1, P]], channel_multiplier=-1).then_inc(masks_step, 1)
            pool.affine_select(out=suffix[:, :], in_=suffix[:, :], compare_op=ALU.is_ge, fill=0.0, base=-1,
                               pattern=[[-1, P]], channel_multiplier=1).then_inc(masks_step, 1)
            pool.memset(xdt[:, :, :], 0.0).then_inc(zeros_ready, 1)
            pool.memset(btok[:, :, :], 0.0).then_inc(zeros_ready, 1)

            for i, (nat, q, arrived) in enumerate(((gate_nat, gate_q, gate_in), (up_nat, up_q, up_in),
                                                   (down_nat, down_q, down_in))):
                pool.wait_ge(magic_ready, i + 1)
                pool.wait_ge(arrived, 16)
                pool.tensor_tensor(nat, nat, magic, ALU.add).then_inc(added, 1)
                pool.wait_ge(added, i + 1)
                pool.tensor_tensor(q[:, :, :].rearrange("p k i -> p (k i)"), nat, magic,
                                   ALU.subtract).then_inc(ffn_q_ready, 1)

            def segments(b):
                for m in range(NM):
                    pool.wait_ge(cs_spread[m], 32 * (b + 1))
                    pool.wait_ge(cs_s_ready, 4 * (b + 1))
                    seg = mix[:, m * GM:(m + 1) * GM, :].rearrange("p g (c l) -> p (g c) l", l=LC)
                    at_s = cs_s[:, m * GM:(m + 1) * GM, :].rearrange("p g c -> p (g c)")
                    pool.tensor_tensor(seg, seg, at_s.unsqueeze(2).broadcast_to([P, GM * NC, LC]),
                                       ALU.subtract).then_inc(seg_ready, 1)

            def fuse_low(b):
                for i in range(NI):
                    pool.wait_ge(hi_ready, b * NI + i + 1)
                    pool.tensor_tensor(fuse_lo[:, i, :], fuse[:, i % 2, :], fuse_hi[:, i, :].bitcast(F32),
                                       ALU.subtract).then_inc(lo_ready, 1)

            def sum_squares(b):
                for m in range(NM):
                    pool.wait_ge(square_ready, b * NM + m + 1)
                    if m == 0:
                        continue
                    if m > 1:
                        pool.wait_ge(sqsum_ready, b * (NM - 1) + m - 1)
                    pool.tensor_tensor(sqsum[:, :], ytmp[:, 0, :] if m == 1 else sqsum[:, :],
                                       ytmp[:, m % 2, :], ALU.add).then_inc(sqsum_ready, 1)

            def add_x(b):
                for t in range(NT):
                    pool.wait_ge(ffn_out, b * NT + t + 1)
                    pool.tensor_tensor(res[:, t, :], res[:, t, :], x_sb[:, b * NT + t, :],
                                       ALU.add).then_inc(ffn_res, 1)

            for b in range(NB):
                segments(b)
                fuse_low(b)
                sum_squares(b)
                add_x(b)

        @block.tensor
        def _(pe):
            def claim(name, b=0):
                k, before, _ = JOB[name, b]
                if before:
                    pe.wait_ge(*read_out(*before))
                return bank[k]

            def fill(name, b=0):
                return full[JOB[name, b][0]]

            def turn(dst, src, n):
                return pe.transpose(dst, src, ident[0:n, 0:n])

            pe.wait_ge(ident_ready, 1)
            for name, arrived, count, blocks in (("w_a", w_a_in, 16, range(4, 8)), ("w_b", w_b_in, 32, (8, 9, 10)),
                                                 ("w_c", w_c_in, 16, range(0, 4))):
                pe.wait_ge(arrived, count)
                for k in range(KT):
                    to = claim(f"{name}{k}")
                    for n, r in enumerate(blocks):
                        rows = P if r < 10 else H
                        src = w_nat[:, r, k * P:(k + 1) * P] if r < 10 else w_dt_nat[0:H, k * P:(k + 1) * P]
                        last = turn(to[:, n * P:n * P + rows], src, rows)
                    last.then_inc(fill(f"{name}{k}"), 1)

            def project_xn(b):
                for k in range(KT):
                    to = claim(f"xn_{k}", b)
                    for t in range(NT):
                        pe.wait_ge(xn_ready, b * NT + t + 1)
                        last = turn(to[:, t * P:(t + 1) * P], xn[:, t, k * P:(k + 1) * P], P)
                    last.then_inc(fill(f"xn_{k}", b), 1)

            def in_projection(name, b, col):
                to = claim(name, b)
                ops = [(w, a, k) for w, a in ((w_hi, xn_hi), (w_lo, xn_hi), (w_hi, xn_lo)) for k in range(KT)]
                for n, (w, a, k) in enumerate(ops):
                    last = pe.matmul(to[:, :], w[:, k, col:col + P], a[:, k, :],
                                     start=(n == 0), stop=(n == len(ops) - 1))
                last.then_inc(fill(name, b), 1)

            def gate_up(n, b):
                q = gate_q if n % 2 == 0 else up_q
                pe.wait_ge(ffn_q_ready, 1 + n % 2)
                to = claim(f"gu_{n}", b)
                i = n // 2
                for k, part in [(k, part) for part in (xn_hi, xn_lo) for k in range(KT)]:
                    last = pe.matmul(to[:, :], q[:, k, i * P:(i + 1) * P], part[:, k, :],
                                     start=(part is xn_hi and k == 0), stop=(part is xn_lo and k == KT - 1))
                last.then_inc(fill(f"gu_{n}", b), 1)

            def down(n, b):
                to = claim(f"down_{n}", b)
                pe.wait_ge(ffn_q_ready, 3)
                pe.wait_ge(lo_ready, NI * (b + 1))
                first = True
                for i in range(NI):
                    for half in range(2):
                        t = 2 * n + half
                        for part in (fuse_hi, fuse_lo):
                            last = pe.matmul(to[:, half * DIM:(half + 1) * DIM], part[:, i, t * P:(t + 1) * P],
                                             down_q[:, i, :], start=first, stop=(i == NI - 1 and part is fuse_lo),
                                             skip_group_check=True)
                            first = False
                last.then_inc(fill(f"down_{n}", b), 1)

            parts = (da_hi, da_mid, da_lo)

            def sums_of_da(b):
                to = claim("cs", b)
                pe.wait_ge(masks_ready, 7)
                pe.wait_ge(da_split, b + 1)
                for t in range(NT):
                    for n, part in enumerate(parts):
                        pe.matmul(to[:, t * H:(t + 1) * H], tri[:, :], part[:, t, :], start=(n == 0), stop=(n == 2))
                for t in range(NT):
                    for n, part in enumerate(parts):
                        pe.matmul(to[:, P + t * H:P + (t + 1) * H], suffix[:, :], part[:, t, :],
                                  start=(n == 0), stop=(n == 2))
                for c in range(NC):
                    for n, part in enumerate(parts):
                        last = pe.matmul(to[:, 2 * P + c * H:2 * P + (c + 1) * H], whole[:, c % 2, :],
                                         part[:, c // 2, :], start=(n == 0), stop=(n == 2))
                last.then_inc(fill("cs", b), 1)
                to = claim("csT", b)
                for t in range(NT):
                    for n, part in enumerate(parts):
                        last = pe.matmul(to[0:H, t * P:(t + 1) * P], part[:, t, :], tri[:, :],
                                         start=(n == 0), stop=(n == 2))
                last.then_inc(fill("csT", b), 1)

            def chunk_state(c, b):
                to = claim(f"s_{c}", b)
                pe.wait_ge(btok_ready, b * NC + c + 1)
                pe.wait_ge(xw_ready, b * NT + c // 2 + 1)
                pe.matmul(to[:, :], btok[:, c, :], xw[:, c // 2, :], start=True,
                          stop=True).then_inc(fill(f"s_{c}", b), 1)

            def from_state(c, b):
                to = claim(f"inter_{c // 2}", b) if c % 2 == 0 or c == 1 else bank_of(f"inter_{c // 2}", b)
                pe.wait_ge(state_ready, b * (NC - 1) + c)
                e = c % 2
                pe.matmul(to[e * LC:(e + 1) * LC, :], xbc[:, 5, c * LC:(c + 1) * LC], state[:, c % 2, :],
                          start=True, stop=True).then_inc(inter_done, 1)

            def within_chunks(m, b):
                to = claim(f"y_{m}", b)
                pe.wait_ge(xdt_ready, 4 * NT * (b + 1))
                for t in range(NT):
                    pe.wait_ge(inter_ready, b * (NT + 0) + t + 1)
                    pe.matmul(to[:, t * P:(t + 1) * P], inter[:, t, m * P:(m + 1) * P], ident[:, :],
                              start=True, stop=False, skip_group_check=True)
                    if t == 0:
                        pe.wait_ge(mix_ready, b * NM + m + 1)
                    for c in (2 * t, 2 * t + 1):
                        for i in range(GM):
                            g = m * GM + i
                            last = pe.matmul(to[32 * i:32 * (i + 1), c * LC:(c + 1) * LC],
                                             xdt[:, c, 32 * g:32 * (g + 1)], mix[:, g, c * LC:(c + 1) * LC],
                                             start=False, stop=True, skip_group_check=True)
                last.then_inc(fill(f"y_{m}", b), 1)

            def out_projection(m, b):
                pe.wait_ge(y_ready, b * NM + m + 1)
                if m == 0:
                    pe.wait_ge(wo_ready, NM)
                for n in range(2):
                    to = claim(f"out_{n}", b) if m == 0 else bank_of(f"out_{n}", b)
                    for half in range(2):
                        t = 2 * n + half
                        last = pe.matmul(to[:, half * DIM:(half + 1) * DIM], sz[:, m, t * P:(t + 1) * P],
                                         woT[:, m, :], start=(m == 0 and half == 0), stop=(m == NM - 1),
                                         skip_group_check=True)
                    if m == NM - 1:
                        last.then_inc(fill(f"out_{n}", b), 1)

            for b in range(NB):
                project_xn(b)
                if b == 0:
                    pe.wait_ge(w_out_in, 16)
                    for n in range(2):
                        to = claim(f"wo_{n}")
                        for i in range(2):
                            for r in range(2):
                                m = 2 * n + i
                                last = turn(to[:, i * DIM + r * P:i * DIM + (r + 1) * P],
                                            wo_nat[:, r, m * P:(m + 1) * P], P)
                        last.then_inc(fill(f"wo_{n}"), 1)
                    pe.wait_ge(w_lo_ready, 4)
                pe.wait_ge(xn_lo_ready, KT * (b + 1))
                in_projection("dt", b, 2 * HID + 2 * NS + H - P)
                for i in CONV_ORDER:
                    in_projection(f"conv_{i}", b, HID + i * P)
                to = claim("dtok", b)
                pe.wait_ge(da_ready, b + 1)
                for t in range(NT):
                    last = pe.transpose(to[:, t * 2 * H:(t + 1) * 2 * H], dtA[2 * H:4 * H, t * P:(t + 1) * P],
                                        ident[2 * H:4 * H, 2 * H:4 * H])
                last.then_inc(fill("dtok", b), 1)
                if b == 0:
                    pe.wait_ge(w_lo_ready, 6)
                in_projection("z_0", b, 0)
                in_projection("z_1", b, P)
                sums_of_da(b)
                in_projection("z_2", b, 2 * P)
                in_projection("z_3", b, 3 * P)
                to = claim("cb", b)
                pe.wait_ge(silu_done, b * NV + 2)
                for c in range(NC):
                    for j in range(2):
                        last = pe.matmul(to[j * LC:(j + 1) * LC, c * LC:(c + 1) * LC],
                                         xbc[:, 4, c * LC:(c + 1) * LC], xbc[:, 5, c * LC:(c + 1) * LC],
                                         start=True, stop=True)
                last.then_inc(fill("cb", b), 1)
                pe.wait_ge(silu_done, b * NV + NV)
                for t in range(NT):
                    to = claim(f"xtok_{t}", b)
                    for m in range(NM):
                        last = turn(to[:, m * P:(m + 1) * P], xbc[:, m, t * P:(t + 1) * P], P)
                    last.then_inc(fill(f"xtok_{t}", b), 1)
                to = claim("btok", b)
                for t in range(NT):
                    last = turn(to[:, t * P:(t + 1) * P], xbc[:, 4, t * P:(t + 1) * P], P)
                last.then_inc(fill("btok", b), 1)
                gate_up(0, b)
                gate_up(1, b)
                chunk_state(0, b)
                chunk_state(1, b)
                n = 2
                for c in range(1, NC):
                    for _i in range(2 if c < 4 else 1):
                        if n < 2 * NI:
                            gate_up(n, b)
                            n += 1
                    from_state(c, b)
                    if c + 1 < NC - 1:
                        chunk_state(c + 1, b)
                while n < 2 * NI:
                    gate_up(n, b)
                    n += 1
                within_chunks(0, b)
                within_chunks(1, b)
                out_projection(0, b)
                down(0, b)
                within_chunks(2, b)
                out_projection(1, b)
                down(1, b)
                within_chunks(3, b)
                out_projection(2, b)
                out_projection(3, b)
                to = claim("ssq", b)
                pe.wait_ge(sqsum_ready, (NM - 1) * (b + 1))
                for t in range(NT):
                    last = pe.matmul(to[:, t:t + 1], sqsum[:, t * P:(t + 1) * P], ones[:, :], start=True, stop=True)
                last.then_inc(fill("ssq", b), 1)

        @block.scalar
        def _(act):
            act.wait_ge(params_in, 16 * N_PARAMS)
            act.activation(heads[3 * H:4 * H, 2:3], heads[3 * H:4 * H, 1:2], ACT.Exp).then_inc(a_exp, 1)

            def layer_norm(b):
                act.wait_ge(meanvar_done, NT * (b + 1))
                act.activation(std[:, :], meanvar[:, :, 1], ACT.Sqrt, bias=eps[:, 0:1]).then_inc(std_ready, 1)

            def weights_high():
                for n, (name, col, width) in enumerate((("w_a", HID, 512), ("w_b", HID + 512, 2 * P + H), ("w_c", 0, 512))):
                    for k in range(KT):
                        src = wait_filled(act, f"{name}{k}")
                        act.activation(w_hi[:, k, col:col + width], src[:, 0:width],
                                       ACT.Copy).then_inc(w_hi_ready, 1)

            def xn_high(b):
                for k in range(KT):
                    src = wait_filled(act, f"xn_{k}", b)
                    if b:
                        wait_filled(act, f"gu_{2 * NI - 1}", b - 1)
                    act.activation(xn_hi[:, k, :], src[:, :], ACT.Copy).then_inc(xn_hi_ready, 1)

            def time_steps(b):
                src = wait_filled(act, "dt", b)
                if b:
                    wait_filled(act, "dtok", b - 1)
                act.activation(dtA[3 * H:4 * H, :], src[3 * H:4 * H, :], ACT.Exp,
                               bias=heads[3 * H:4 * H, 0:1]).then_inc(dt_exp, 1)
                act.wait_ge(dt_exp, b + 1)
                act.activation(dtA[3 * H:4 * H, :], dtA[3 * H:4 * H, :], ACT.Ln, bias=1.0).then_inc(dt_ln, 1)

            def last_tap(i, b):
                src = wait_filled(act, f"conv_{i}", b)
                if b and i == 4:
                    act.wait_ge(inter_done, (NC - 1) * b)
                    act.wait_ge(skip_added, NM * b)
                act.activation(xbc[:, i, :], src[:, :], ACT.Identity, bias=convb[:, i:i + 1],
                               scale=convw[:, i, TAPS - 1:TAPS]).then_inc(tap_done, 1)

            def silu_conv(n, i, b):
                act.wait_ge(conv_done, b * NV + n + 1)
                act.activation(xbc[:, i, :], xbc[:, i, :], ACT.Silu).then_inc(silu_done, 1)

            def decays(b):
                src = wait_filled(act, "csT", b)
                if b:
                    act.wait_ge(cs_stored, 16 * b)
                act.activation(csT[:, :], src[0:H, :], ACT.Copy).then_inc(csT_ready, 1)
                act.wait_ge(csT_ready, b + 1)
                src = wait_filled(act, "cs", b)
                if b:
                    act.wait_ge(inter_ready, NT * b)
                    act.wait_ge(state_ready, (NC - 1) * b)
                    act.wait_ge(xw_ready, NT * b)
                act.activation(decay_in[:, :, :], src[:, 0:P].rearrange("p (t h) -> p t h", h=H),
                               ACT.Exp).then_inc(decays_ready, 1)
                act.activation(decay_out[:, :, :], src[:, P:2 * P].rearrange("p (t h) -> p t h", h=H),
                               ACT.Exp).then_inc(decays_ready, 1)
                act.activation(decay_all[:, :, :], src[:, 2 * P:4 * P].rearrange("p (c h) -> p c h", h=H),
                               ACT.Exp).then_inc(decays_ready, 1)

            def silu_z(i, b):
                src = wait_filled(act, f"z_{i}", b)
                if b:
                    wait_filled(act, "out_1", b - 1)
                    act.wait_ge(square_ready, NM * b)
                act.activation(sz[:, i, :], src[:, :], ACT.Silu).then_inc(sz_ready, 1)

            def exp_segments(m, b):
                act.wait_ge(seg_capped, b * NM + m + 1)
                seg = mix[:, m * GM:(m + 1) * GM, :]
                act.activation(seg, seg, ACT.Exp).then_inc(seg_exp, 1)

            def gate(i, b):
                src = wait_filled(act, f"gu_{2 * i}", b)
                if b * NI + i >= 2:
                    act.wait_ge(lo_ready, b * NI + i - 1)
                act.activation(fuse[:, i % 2, :], src[:, :], ACT.Silu,
                               scale=gscale[:, i:i + 1]).then_inc(gate_ready, 1)

            def fuse_high(i, b):
                act.wait_ge(fuse_ready, b * NI + i + 1)
                if b:
                    wait_filled(act, "down_1", b - 1)
                act.activation(fuse_hi[:, i, :], fuse[:, i % 2, :], ACT.Copy).then_inc(hi_ready, 1)

            def square(m, b):
                act.wait_ge(y_ready, b * NM + m + 1)
                act.activation(ytmp[:, m % 2, :], sz[:, m, :], ACT.Square).then_inc(square_ready, 1)

            def root_mean_square(b):
                src = wait_filled(act, "ssq", b)
                act.activation(rms[:, :], src[:, 0:NT], ACT.Sqrt, scale=1.0 / HID,
                               bias=eps[:, 1:2]).then_inc(rms_ready, 1)

            layer_norm(0)
            weights_high()
            for b in range(NB):
                xn_high(b)
                if b == 0:
                    for m in range(NM):
                        src = wait_filled(act, f"wo_{m // 2}")
                        act.activation(woT[:, m, :], src[:, (m % 2) * DIM:(m % 2 + 1) * DIM], ACT.Copy,
                                       scale=normw[:, m:m + 1]).then_inc(wo_ready, 1)
                time_steps(b)
                for i in CONV_ORDER:
                    last_tap(i, b)
                decays(b)
                for n, i in enumerate(CONV_ORDER):
                    silu_conv(n, i, b)
                for i in range(NM):
                    silu_z(i, b)
                for i in range(NI):
                    gate(i, b)
                    if i:
                        fuse_high(i - 1, b)
                fuse_high(NI - 1, b)
                for m in range(NM):
                    exp_segments(m, b)
                for m in range(NM - 1):
                    square(m, b)
                if b + 1 < NB:
                    layer_norm(b + 1)
                square(NM - 1, b)
                root_mean_square(b)

        @block.vector
        def _(dve):
            dve.memset(eps[:, 0:1], LN_EPS).then_inc(a_neg, 1)
            dve.memset(eps[:, 1:2], RMS_EPS).then_inc(a_neg, 1)

            def masks():
                dve.wait_ge(masks_step, 5)
                dve.memset(whole[0:LC, 0, :], 1.0).then_inc(masks_ready, 1)
                dve.memset(whole[LC:P, 1, :], 1.0).then_inc(masks_ready, 1)
                dve.memset(tri[0:LC, LC:P], 0.0).then_inc(masks_ready, 1)
                dve.memset(suffix[LC:P, 0:LC], 0.0).then_inc(masks_ready, 1)
                for e in range(2):
                    dve.tensor_copy(causal[e * LC:(e + 1) * LC, :],
                                    tri[e * LC:(e + 1) * LC, e * LC:(e + 1) * LC]).then_inc(masks_ready, 1)
                dve.memset(ones[:, :], 1.0).then_inc(masks_ready, 1)

            def layer_norm(b):
                for t in range(NT):
                    n = b * NT + t
                    dve.wait_ge(x_in[n], 16)
                    dve.bn_stats(stats[:, t, :], x_sb[:, n, :]).then_inc(stats_done, 1)
                for t in range(NT):
                    dve.wait_ge(stats_done, b * NT + t + 1)
                    dve.bn_aggr(meanvar[:, t, :], stats[:, t, :]).then_inc(meanvar_done, 1)
                dve.wait_ge(std_ready, b + 1)
                dve.reciprocal(rstd[:, :], std[:, :]).then_inc(rstd_ready, 1)
                dve.wait_ge(rstd_ready, b + 1)
                if b:
                    wait_filled(dve, "xn_1", b - 1)
                for t in range(NT):
                    dve.tensor_scalar(xn[:, t, :], x_sb[:, b * NT + t, :], meanvar[:, t, 0:1], rstd[:, t:t + 1],
                                      ALU.subtract, ALU.mult).then_inc(xn_ready, 1)

            def weights_low(name, n, col, width):
                for k in range(KT):
                    src = wait_filled(dve, f"{name}{k}")
                    dve.wait_ge(w_hi_ready, n + k + 1)
                    dve.tensor_tensor(w_lo[:, k, col:col + width], src[:, 0:width],
                                      w_hi[:, k, col:col + width].bitcast(F32),
                                      ALU.subtract).then_inc(w_lo_ready, 1)

            def magic_numbers(i, nat, arrived):
                dve.wait_ge(arrived, 16)
                if i:
                    dve.wait_ge(ffn_q_ready, i)
                dve.tensor_scalar(magic.bitcast(U32), nat.bitcast(U32), EXPONENT, None,
                                  ALU.bitwise_and).then_inc(expo_step, 1)
                dve.wait_ge(expo_step, i + 1)
                dve.tensor_scalar(magic, magic, E4M3_MIN_NORMAL, ROUND_TO_E4M3, ALU.max,
                                  ALU.mult).then_inc(magic_ready, 1)

            def xn_low(b):
                for k in range(KT):
                    src = wait_filled(dve, f"xn_{k}", b)
                    dve.wait_ge(xn_hi_ready, b * KT + k + 1)
                    dve.tensor_tensor(xn_lo[:, k, :], src[:, :], xn_hi[:, k, :].bitcast(F32),
                                      ALU.subtract).then_inc(xn_lo_ready, 1)

            def time_steps(b):
                dve.wait_ge(dt_ln, b + 1)
                dt = dtA[3 * H:4 * H, :]
                dve.tensor_scalar(dt, dt, DT_MIN, DT_MAX, ALU.max, ALU.min).then_inc(dt_clipped, 1)
                dve.wait_ge(dt_clipped, b + 1)
                dve.tensor_scalar(dtA[2 * H:3 * H, :], dt, heads[3 * H:4 * H, 3:4], None,
                                  ALU.mult).then_inc(da_ready, 1)

            def other_taps(n, i, b):
                src = bank_of(f"conv_{i}", b)
                for k in range(1, TAPS):
                    dve.wait_ge(tap_done, b * NV + n + 1)
                    if k > 1:
                        dve.wait_ge(tap_step, (b * NV + n) * (TAPS - 2) + k - 1)
                    done = tap_step if k < TAPS - 1 else conv_done
                    dve.scalar_tensor_tensor(out=xbc[:, i, k:S], in0=src[:, 0:S - k],
                                             scalar=convw[:, i, TAPS - 1 - k:TAPS - k], in1=xbc[:, i, k:S],
                                             op0=ALU.mult, op1=ALU.add).then_inc(done, 1)

            def split_da(b):
                src = wait_filled(dve, "dtok", b)[:, 0:NT * 2 * H].rearrange("p (t h) -> p t h", h=2 * H)
                if b:
                    wait_filled(dve, "csT", b - 1)
                da = src[:, :, 0:H]
                n = 3 * b
                dve.tensor_copy(dtok[:, :, :], src[:, :, H:2 * H]).then_inc(dtok_copied, 1)
                dve.tensor_copy(da_hi[:, :, :], da).then_inc(dtok_step, 1)
                dve.wait_ge(dtok_step, n + 1)
                dve.tensor_tensor(rest1[:, :, :], da, da_hi[:, :, :], ALU.subtract).then_inc(dtok_step, 1)
                dve.wait_ge(dtok_step, n + 2)
                dve.tensor_copy(da_mid[:, :, :], rest1[:, :, :]).then_inc(dtok_step, 1)
                dve.wait_ge(dtok_step, n + 3)
                dve.tensor_tensor(da_lo[:, :, :], rest1[:, :, :], da_mid[:, :, :], ALU.subtract).then_inc(da_split, 1)

            def chunk_sums(b):
                src = bank_of("cs", b)
                dve.wait_ge(decays_ready, 3 * (b + 1))
                if b:
                    dve.wait_ge(seg_ready, NM * b)
                for j in range(2):
                    for e in range(2):
                        dve.tensor_copy(
                            cs_s[j * LC:(j + 1) * LC, :, e:NC:2].rearrange("p g t -> p t g"),
                            src[e * LC:(e + 1) * LC, 0:P].rearrange("p (t g j) -> p t g j", t=NT, j=2)[:, :, :, j],
                        ).then_inc(cs_s_ready, 1)
                dve.wait_ge(dtok_copied, b + 1)
                dve.tensor_tensor(decay_out[:, :, :], decay_out[:, :, :], dtok[:, :, :],
                                  ALU.mult).then_inc(decay_out_ready, 1)

            def by_head(ap, shape):
                return ap.unsqueeze(2).broadcast_to(shape)

            def tokens(b):
                src = wait_filled(dve, "cb", b)
                dve.wait_ge(masks_ready, 7)
                if b:
                    dve.wait_ge(mix_ready, NM * b)
                dve.tensor_tensor(cbm[:, :, :], src[:, :].rearrange("p (c l) -> p c l", l=LC),
                                  causal[:, :].unsqueeze(1).broadcast_to([P, NC, LC]),
                                  ALU.mult).then_inc(cbm_ready, 1)
                dve.wait_ge(zeros_ready, 2)
                dve.wait_ge(decay_out_ready, b + 1)
                if b == 0:
                    dve.wait_ge(ffn_q_ready, 2)
                else:
                    wait_filled(dve, "y_3", b - 1)
                    wait_filled(dve, f"s_{NC - 2}", b - 1)
                for t in range(NT):
                    src = wait_filled(dve, f"xtok_{t}", b)
                    dve.tensor_tensor(xw[:, t, :].rearrange("p (h q) -> p h q", q=HP),
                                      src[:, :].rearrange("p (h q) -> p h q", q=HP),
                                      by_head(decay_out[:, t, :], [P, H, HP]), ALU.mult).then_inc(xw_ready, 1)
                    for e in range(2):
                        rows = slice(e * LC, (e + 1) * LC)
                        for j in range(2):
                            ins = dve.tensor_tensor(
                                xdt[j * LC:(j + 1) * LC, 2 * t + e, :].rearrange("p (g j q) -> p g j q", j=2, q=HP)[:, :, j, :],
                                src[rows, :].rearrange("p (g j q) -> p g j q", j=2, q=HP)[:, :, j, :],
                                by_head(dtok[rows, t, j:H:2], [LC, NG, HP]), ALU.mult)
                            ins.then_inc(xdt_ready, 1)
                src = wait_filled(dve, "btok", b)
                for c in range(NC):
                    rows = slice((c % 2) * LC, (c % 2 + 1) * LC)
                    dve.tensor_copy(btok[rows, c, :], src[rows, (c // 2) * P:(c // 2 + 1) * P]).then_inc(btok_ready, 1)

            def next_state(c, b):
                src = wait_filled(dve, f"s_{c}", b)
                new = state[:, (c + 1) % 2, :]
                if c >= 2:
                    dve.wait_ge(inter_done, b * (NC - 1) + c - 1)
                elif b:
                    dve.wait_ge(inter_done, b * (NC - 1))
                n = b * (NC - 1) + c
                if c == 0:
                    dve.tensor_copy(new, src[:, :]).then_inc(state_ready, 1)
                else:
                    dve.wait_ge(state_ready, n)
                    dve.tensor_tensor(new.rearrange("p (h q) -> p h q", q=HP),
                                      state[:, c % 2, :].rearrange("p (h q) -> p h q", q=HP),
                                      by_head(decay_all[:, c, :], [P, H, HP]), ALU.mult).then_inc(state_scaled, 1)
                    dve.wait_ge(state_scaled, b * (NC - 2) + c)
                    dve.tensor_tensor(new, new, src[:, :], ALU.add).then_inc(state_ready, 1)

            def scale_inter(t, b):
                dve.wait_ge(inter_done, b * (NC - 1) + 2 * t + 1)
                if b and t == 0:
                    wait_filled(dve, "y_3", b - 1)
                if t == 0:
                    dve.memset(inter[0:LC, 0, :], 0.0).then_inc(inter_zero, 1)
                    dve.wait_ge(inter_zero, b + 1)
                rows = slice(LC if t == 0 else 0, P)
                n = P - rows.start
                src = bank_of(f"inter_{t}", b)
                dve.tensor_tensor(inter[rows, t, :].rearrange("p (h q) -> p h q", q=HP),
                                  src[rows, :].rearrange("p (h q) -> p h q", q=HP),
                                  by_head(decay_in[rows, t, :], [n, H, HP]), ALU.mult).then_inc(inter_ready, 1)

            def fuse_up(i, b):
                src = wait_filled(dve, f"gu_{2 * i + 1}", b)
                dve.wait_ge(gate_ready, b * NI + i + 1)
                dve.scalar_tensor_tensor(out=fuse[:, i % 2, :], in0=src[:, :], scalar=uscale[:, i:i + 1],
                                         in1=fuse[:, i % 2, :], op0=ALU.mult, op1=ALU.mult).then_inc(fuse_ready, 1)

            def cap_segments(m, b):
                dve.wait_ge(seg_ready, b * NM + m + 1)
                seg = mix[:, m * GM:(m + 1) * GM, :]
                dve.tensor_scalar(seg, seg, 0.0, None, ALU.min).then_inc(seg_capped, 1)

            def mix_group(m, b):
                dve.wait_ge(seg_exp, b * NM + m + 1)
                if m == 0:
                    dve.wait_ge(cbm_ready, b + 1)
                seg = mix[:, m * GM:(m + 1) * GM, :]
                cb = cbm[:, :, :].rearrange("p c l -> p (c l)")
                dve.tensor_tensor(seg, seg, cb.unsqueeze(1).broadcast_to([P, GM, S]),
                                  ALU.mult).then_inc(mix_ready, 1)

            def gated(m, b):
                src = wait_filled(dve, f"y_{m}", b)
                n = b * NM + m
                if m >= 2:
                    dve.wait_ge(sqsum_ready, b * (NM - 1) + m - 1)
                elif b:
                    dve.wait_ge(sqsum_ready, b * (NM - 1))
                dve.scalar_tensor_tensor(out=ytmp[:, m % 2, :], in0=xbc[:, m, :], scalar=dcol[:, m:m + 1],
                                         in1=src[:, :], op0=ALU.mult, op1=ALU.add).then_inc(skip_added, 1)
                dve.wait_ge(skip_added, n + 1)
                dve.wait_ge(sz_ready, n + 1)
                dve.tensor_tensor(sz[:, m, :], ytmp[:, m % 2, :], sz[:, m, :], ALU.mult).then_inc(y_ready, 1)

            def ffn_result(b):
                for t in range(NT):
                    src = wait_filled(dve, f"down_{t // 2}", b)
                    if b:
                        dve.wait_ge(stored, 16 * NT * b)
                    dve.tensor_tensor(res[:, t, :], src[:, (t % 2) * DIM:(t % 2 + 1) * DIM], dscale[:, :],
                                      ALU.mult).then_inc(ffn_out, 1)

            def result(b):
                dve.wait_ge(rms_ready, b + 1)
                dve.reciprocal(rrms[:, :], rms[:, :]).then_inc(rrms_ready, 1)
                dve.wait_ge(rrms_ready, b + 1)
                for t in range(NT):
                    src = wait_filled(dve, f"out_{t // 2}", b)
                    dve.wait_ge(ffn_res, b * NT + t + 1)
                    dve.scalar_tensor_tensor(out=res[:, t, :], in0=src[:, (t % 2) * DIM:(t % 2 + 1) * DIM],
                                             scalar=rrms[:, t:t + 1], in1=res[:, t, :], op0=ALU.mult,
                                             op1=ALU.add).then_inc(res_ready, 1)

            masks()
            layer_norm(0)
            magic_numbers(0, gate_nat, gate_in)
            weights_low("w_a", 0, HID, 512)
            weights_low("w_b", 2, HID + 512, 2 * P + H)
            xn_low(0)
            weights_low("w_c", 4, 0, 512)
            magic_numbers(1, up_nat, up_in)
            dve.wait_ge(a_exp, 1)
            dve.tensor_scalar(heads[3 * H:4 * H, 3:4], heads[3 * H:4 * H, 2:3], -1.0, None,
                              ALU.mult).then_inc(a_neg, 1)
            dve.wait_ge(a_neg, 3)
            for b in range(NB):
                if b:
                    xn_low(b)
                time_steps(b)
                other_taps(0, 4, b)
                split_da(b)
                other_taps(1, 5, b)
                for n, i in enumerate((0, 1, 2, 3)):
                    other_taps(n + 2, i, b)
                chunk_sums(b)
                if b == 0:
                    magic_numbers(2, down_nat, down_in)
                tokens(b)
                next_state(0, b)
                for c in range(1, NC):
                    if c - 1 < NI:
                        fuse_up(c - 1, b)
                    if c < NC - 1:
                        next_state(c, b)
                    if c % 2:
                        scale_inter(c // 2, b)
                for m in range(NM):
                    cap_segments(m, b)
                for m in range(2):
                    mix_group(m, b)
                gated(0, b)
                mix_group(2, b)
                gated(1, b)
                mix_group(3, b)
                ffn_result(b)
                gated(2, b)
                if b + 1 < NB:
                    layer_norm(b + 1)
                gated(3, b)
                result(b)




_INS = ['L0_attn_x', 'L0_attn_W_in', 'L0_attn_conv_w', 'L0_attn_conv_b', 'L0_attn_dt_bias', 'L0_attn_A_log',
        'L0_attn_D', 'L0_attn_norm_w', 'L0_attn_W_out', 'L0_ffn_gate_w', 'L0_ffn_up_w', 'L0_ffn_down_w',
        'L0_ffn_gate_scale', 'L0_ffn_up_scale', 'L0_ffn_down_scale']


def kernel(**inputs):
    import numpy as _np
    import concourse.bacc as _bacc
    from concourse import mybir as _mybir
    from concourse.bass_utils import run_bass_kernel_spmd as _run

    nc = _bacc.Bacc("TRN2", target_bir_lowering=False, num_devices=1)
    arrays, args = {}, []
    for name in _INS:
        a = _np.ascontiguousarray(inputs[name])
        arrays[f"in_{name}"] = a
        args.append(nc.dram_tensor(f"in_{name}", a.shape, _mybir.dt.from_np(a.dtype), kind="ExternalInput").ap())
    shape = inputs['L0_attn_x'].shape
    args.append(nc.dram_tensor("out_0", shape, _mybir.dt.float32, kind="ExternalOutput").ap())
    mamba_and_ffn_block(nc, *args)
    r = _run(nc, [arrays], core_ids=[0])
    return r.results[0]["out_0"]
```

```python
from contextlib import ExitStack

import concourse.bass as bass
from concourse import mybir

ALU = mybir.AluOpType
ACT = mybir.ActivationFunctionType
F32 = mybir.dt.float32
F32R = mybir.dt.float32r
BF16 = mybir.dt.bfloat16
U32 = mybir.dt.uint32

P = 128
LC = 64
NS = 128
HP = 16
LN_EPS = 1e-5
RMS_EPS = 1e-6
DT_MIN, DT_MAX = 0.001, 0.1
EXPONENT = 0x7F800000
E4M3_MIN_NORMAL = 2.0 ** -6
ROUND_TO_E4M3 = 1.5 * 2.0 ** 20

CONV_ORDER = (4, 5, 0, 1, 2, 3)

FFN0 = range(0, 12)
FFN1 = range(12, 24)
BANKS = [
    [("xn_0", 0), ("w_c0", 0), ("conv_3", 0), ("xn_0", 1), ("dt", 1), ("dtok", 1), ("csT", 1)]
    + [("xtok", n) for n in range(8)],
    [("xn_1", 0), ("w_c1", 0), ("cs", 0), ("xn_1", 1), ("cs", 1)] + [("btcb", n) for n in range(8)],
    [("w_b0", 0), ("dt", 0), ("dtok", 0), ("csT", 0)] + [("gu", k) for k in FFN0 if k % 2]
    + [("s", c) for c in range(16) if c % 8 != 7],
    [("w_b1", 0), ("conv_4", 0), ("z_0", 0), ("conv_4", 1), ("conv_1", 1), ("z_0", 1), ("z_3", 1)]
    + [("inter", n) for n in range(8)],
    [("w_a0", 0), ("conv_5", 0), ("z_1", 0), ("conv_5", 1), ("conv_2", 1), ("z_1", 1)] + [("y", n) for n in range(8)],
    [("w_a1", 0), ("conv_0", 0), ("z_2", 0), ("conv_0", 1), ("conv_3", 1), ("z_2", 1)] + [("out", n) for n in range(8)],
    [("wo_0", 0), ("conv_1", 0), ("z_3", 0)] + [("gu", k) for k in FFN0 if k % 2 == 0] + [("gu", k) for k in FFN1],
    [("wo_1", 0), ("conv_2", 0)] + [("down", h) for h in range(4)],
]


def number_jobs():
    found = {}
    for k, users in enumerate(BANKS):
        before, fills = None, 0
        for job in users:
            fills += job[0] not in ("inter", "down")
            found[job] = k, before, fills
            before = job
    return found


def mamba_and_ffn_block(nc, x, w_in, conv_w, conv_b, dt_bias, a_log, d_skip, norm_w, w_out,
                        gate_w, up_w, down_w, gate_scale, up_scale, down_scale, out):
    NB, S, DIM = x.shape
    H = a_log.shape[0]
    HID = norm_w.shape[0]
    CONV = conv_w.shape[0]
    I = gate_w.shape[1]
    TAPS = conv_w.shape[1]
    NT = S // P
    NN = NB * NT
    NC = S // LC
    KT = DIM // P
    NM = HID // P
    NV = CONV // P
    NI = I // P
    NG = H // 2
    GM = NG // NM
    SH = S // 2
    NP = NI * 2 * NB
    JOB = number_jobs()

    with ExitStack() as ctx:
        def sb(name, shape, dt=F32):
            return ctx.enter_context(nc.sbuf_tensor(name, shape, dt))

        def sem(name):
            return ctx.enter_context(nc.semaphore(name))

        bank = [ctx.enter_context(nc.psum_tensor(f"bank{i}", [P, 512], F32)) for i in range(8)]
        cs_dram = nc.dram_tensor("cs_scratch", [NB, H, S], F32).ap()

        ident = sb("ident", [P, P])
        tri = sb("tri", [P, P], BF16)
        suffix = sb("suffix", [P, P], BF16)
        whole = sb("whole", [P, 2, P], BF16)
        causal = sb("causal", [P, LC])
        ones = sb("ones", [P, 1])
        minus_half = sb("minus_half", [P, NT])
        convw = sb("convw", [P, NV, TAPS])
        convb = sb("convb", [P, NV])
        heads = sb("heads", [P, 4])
        dcol = sb("dcol", [P, NM])
        normw = sb("normw", [P, NM])
        gscale = sb("gscale", [P, NI])
        uscale = sb("uscale", [P, NI])
        dscale = sb("dscale", [P, DIM])
        w_hi = sb("w_hi", [P, KT, 2 * HID + 2 * NS + H], F32R)
        w_lo = sb("w_lo", [P, KT, 2 * HID + 2 * NS + H], F32R)
        woT = sb("woT", [P, NM, DIM])
        diag_d = sb("diag_d", [P, NM, P])
        gate_q = sb("gate_q", [P, KT, I], F32R)
        up_q = sb("up_q", [P, KT, I], F32R)
        down_q = sb("down_q", [P, NI, DIM], F32R)
        x_sb = sb("x_sb", [P, NN, DIM])
        stats = sb("stats", [P, NT, 6])
        meanvar = sb("meanvar", [P, NT, 2])
        var_eps = sb("var_eps", [P, NT])
        rstd = sb("rstd", [P, NT])
        xn = sb("xn", [P, NT, DIM])
        xn_hi = sb("xn_hi", [P, NB, KT, S], F32R)
        xn_lo = sb("xn_lo", [P, NB, KT, S], F32R)
        xbc = sb("xbc", [P, NB, NV, S])
        sz = sb("sz", [P, NB, NM, S])
        dtA = sb("dtA", [P, S])
        csT = sb("csT", [H, S])
        dtok = sb("dtok", [P, NB, NT, H])
        rest1 = sb("rest1", [P, NT, H])
        da_hi = sb("da_hi", [P, NT, H], BF16)
        da_mid = sb("da_mid", [P, NT, H], BF16)
        da_lo = sb("da_lo", [P, NT, H], BF16)
        cs_s = sb("cs_s", [P, NB, NG, NC])
        decay_in = sb("decay_in", [P, NB, NT, H])
        decay_out = sb("decay_out", [P, NB, NT, H])
        decay_all = sb("decay_all", [P, NB, NC, H])
        cbm = sb("cbm", [P, 2, 2, LC])
        mix = sb("mix", [P, 3, NG, P])
        xdiag = sb("xdiag", [P, 2, 2, HID])
        xdt = sb("xdt", [P, 2, HID])
        xw = sb("xw", [P, 2, HID])
        btok = sb("btok", [P, 2, 2, NS])
        state = sb("state", [P, 3, HID])
        inter = sb("inter", [P, 2, HID])
        square = sb("square", [P, NM, P])
        sq2 = sb("sq2", [P, 2, P])
        sqsum = sb("sqsum", [P, P])
        ms = sb("ms", [P, 2])
        rrms = sb("rrms", [P, 2])
        fuse = sb("fuse", [P, 2, SH])
        fuse_hi = sb("fuse_hi", [P, 2, SH], F32R)
        fuse_lo = sb("fuse_lo", [P, 2, SH], F32R)
        ffn = sb("ffn", [P, 2, DIM])

        mix_flat = mix[:, :, :, :].rearrange("p n g t -> p (n g t)")
        w_nat = mix_flat[:, 0:10 * DIM].rearrange("p (r k) -> p r k", k=DIM)
        w_dt_nat = mix_flat[:, 10 * DIM:11 * DIM]
        wo_nat = mix_flat[:, 11 * DIM:11 * DIM + 2 * HID].rearrange("p (r k) -> p r k", k=HID)
        magic = [mix_flat[:, 11 * DIM + 2 * HID:11 * DIM + 2 * HID + KT * I],
                 xdiag[:, :, :, :].rearrange("p n e q -> p (n e q)")[:, 0:KT * I]]
        xbc_flat = xbc[:, 1, :, :].rearrange("p v t -> p (v t)")
        gate_nat = xbc_flat[:, 0:KT * I]
        up_nat = xbc_flat[:, KT * I:2 * KT * I]
        down_nat = sz[:, 1, :, :].rearrange("p m t -> p (m t)")[:, 0:KT * I]

        full = [sem(f"bank{i}_full") for i in range(8)]
        x_in = [sem(f"x_in{h}") for h in range(NN // 2)]
        w_a_in, w_b_in, w_c_in, w_out_in = sem("w_a_in"), sem("w_b_in"), sem("w_c_in"), sem("w_out_in")
        gate_in, up_in, down_in = sem("gate_in"), sem("up_in"), sem("down_in")
        front_params_in, norm_w_in, d_skip_in, scales_in = (
            sem(n) for n in ("front_params_in", "norm_w_in", "d_skip_in", "scales_in"))
        ident_zero, ident_ready = sem("ident_zero"), sem("ident_ready")
        masks_step, masks_ready = sem("masks_step"), sem("masks_ready")
        zeros_ready, half_ready = sem("zeros_ready"), sem("half_ready")
        stats_done, meanvar_done, var_ready, rstd_ready, xn_ready = (
            sem(n) for n in ("stats_done", "meanvar_done", "var_ready", "rstd_ready", "xn_ready"))
        w_hi_ready, w_lo_ready, wo_ready = sem("w_hi_ready"), sem("w_lo_ready"), sem("wo_ready")
        expo_step, magic_ready, added, ffn_q_ready = (
            sem("expo_step"), sem("magic_ready"), sem("added"), sem("ffn_q_ready"))
        xn_hi_ready, xn_lo_ready = sem("xn_hi_ready"), sem("xn_lo_ready")
        dt_exp, dt_ln, dt_clipped, da_ready = sem("dt_exp"), sem("dt_ln"), sem("dt_clipped"), sem("da_ready")
        a_exp, a_neg = sem("a_exp"), sem("a_neg")
        dtok_ready, dtok_step, da_split = sem("dtok_ready"), sem("dtok_step"), sem("da_split")
        csT_ready, cs_stored, decays_ready, cs_s_ready = (
            sem(n) for n in ("csT_ready", "cs_stored", "decays_ready", "cs_s_ready"))
        cs_spread = [sem(f"cs_spread{i}") for i in range(3)]
        tap_done, tap_step, conv_done, silu_done, sz_ready = (
            sem(n) for n in ("tap_done", "tap_step", "conv_done", "silu_done", "sz_ready"))
        cbm_ready, xdt_ready, xdiag_ready, xw_ready, btok_ready, diag_ready = (
            sem(n) for n in ("cbm_ready", "xdt_ready", "xdiag_ready", "xw_ready", "btok_ready", "diag_ready"))
        state_scaled, state_ready, inter_done, inter_zero, inter_ready = (
            sem(n) for n in ("state_scaled", "state_ready", "inter_done", "inter_zero", "inter_ready"))
        seg_ready, seg_capped, seg_exp, mix_ready = (
            sem("seg_ready"), sem("seg_capped"), sem("seg_exp"), sem("mix_ready"))
        gate_ready, fuse_ready, hi_ready, lo_ready, down_done = (
            sem(n) for n in ("gate_ready", "fuse_ready", "hi_ready", "lo_ready", "down_done"))
        y_ready, square_ready, sq2_ready, sqsum_ready = (
            sem(n) for n in ("y_ready", "square_ready", "sq2_ready", "sqsum_ready"))
        ms_ready, rrms_ready, ffn_out, ffn_added, res_ready, stored = (
            sem(n) for n in ("ms_ready", "rrms_ready", "ffn_out", "ffn_added", "res_ready", "stored"))

        def wait_filled(eng, name, n=0):
            k, _, fills = JOB[name, n]
            eng.wait_ge(full[k], fills)
            return bank[k]

        def bank_of(name, n=0):
            return bank[JOB[name, n][0]]

        def states_before(c):
            return c - c // NC

        def wait_states_made(eng, n):
            c = 2 * n + 1 if (2 * n + 1) % NC != NC - 1 else 2 * n
            eng.wait_ge(state_ready, states_before(c) + 1)

        def by_head(ap, shape):
            return ap.unsqueeze(2).broadcast_to(shape)

        def read_out(name, n):
            kind, _, i = name.rpartition("_")
            i = int(i) if i.isdigit() else 0
            return {
                "w": lambda: (w_lo_ready, 1 + ("b0", "b1", "a0", "a1", "c0", "c1").index(name[2:])),
                "wo": lambda: (wo_ready, 2 * i + 2),
                "xn": lambda: (xn_lo_ready, n * KT + i + 1),
                "dt": lambda: (dt_exp, n + 1),
                "conv": lambda: (conv_done, n * NV + CONV_ORDER.index(i) + 1),
                "dtok": lambda: (dtok_step, 3 * n + 2),
                "cs": lambda: (cs_s_ready, 4 * n + 4),
                "csT": lambda: (csT_ready, n + 1),
                "z": lambda: (sz_ready, n * NM + i + 1),
                "gu": lambda: (fuse_ready, n + 1),
                "down": lambda: (ffn_out, 2 * n + 2),
                "xtok": lambda: (xdt_ready, n + 1),
                "btcb": lambda: (cbm_ready, 4 * n + 4),
                "s": lambda: (state_ready, states_before(n) + 1),
                "inter": lambda: (inter_ready, n + 1),
                "y": lambda: (y_ready, n + 1),
                "out": lambda: (res_ready, n + 1),
            }[kind or name]()

        block = ctx.enter_context(nc.Block())

        @block.sync
        def _(sp):
            w_rows = w_in[0:10 * P, :].rearrange("(r p) k -> p r k", p=P)

            def load_x(h):
                b, half = divmod(h, 2)
                sp.dma_start(x_sb[:, 2 * h:2 * h + 2, :],
                             x[b, half * SH:(half + 1) * SH, :].rearrange("(t p) k -> p t k", p=P)).then_inc(x_in[h], 16)

            load_x(0)
            load_x(1)
            sp.dma_start(w_nat[:, 8:10, :], w_rows[:, 8:10, :]).then_inc(w_b_in, 16)
            sp.dma_start(w_dt_nat[0:H, :], w_in[10 * P:10 * P + H, :]).then_inc(w_b_in, 16)
            sp.dma_start(w_nat[:, 4:8, :], w_rows[:, 4:8, :]).then_inc(w_a_in, 16)
            sp.dma_start(gate_nat.rearrange("p (k i) -> p k i", i=I),
                         gate_w.rearrange("(k p) i -> p k i", p=P)).then_inc(gate_in, 16)
            sp.dma_start(wo_nat, w_out.rearrange("(r p) c -> p r c", p=P)).then_inc(w_out_in, 16)
            sp.dma_start(up_nat.rearrange("p (k i) -> p k i", i=I),
                         up_w.rearrange("(k p) i -> p k i", p=P)).then_inc(up_in, 16)
            sp.dma_start(w_nat[:, 0:4, :], w_rows[:, 0:4, :]).then_inc(w_c_in, 16)
            sp.dma_start(down_nat.rearrange("p (k i) -> p k i", i=DIM),
                         down_w.rearrange("(k p) i -> p k i", p=P)).then_inc(down_in, 16)
            with nc.allow_non_contiguous_dma(reason="small parameters"):
                for m in range(NM):
                    sp.dma_start(dcol[:, m:m + 1], bass.AP(tensor=d_skip.tensor, offset=m * (P // HP),
                                                           ap=[[1, P // HP], [0, HP], [1, 1]])).then_inc(d_skip_in, 16)
                sp.dma_start(gscale[:, :], gate_scale.rearrange("(m p) -> p m", p=P)).then_inc(scales_in, 16)
                sp.dma_start(uscale[:, :], up_scale.rearrange("(m p) -> p m", p=P)).then_inc(scales_in, 16)
                sp.dma_start(dscale[:, :], down_scale.partition_broadcast(P)).then_inc(scales_in, 16)
            load_x(2)
            load_x(3)

            def store_cs(b):
                sp.wait_ge(csT_ready, b + 1)
                sp.dma_start(cs_dram[b], csT[:, :]).then_inc(cs_stored, 16)

            def spread_cs(n):
                b, t = divmod(n, NT)
                sp.wait_ge(cs_stored, 16 * (b + 1))
                if n >= 3:
                    wait_filled(sp, "y", n - 3)
                elif n == 0:
                    for name in ("w_a1", "w_b1", "w_c1"):
                        wait_filled(sp, name)
                elif n == 1:
                    wait_filled(sp, "wo_1")
                    sp.wait_ge(ffn_q_ready, 3)
                for j in range(2):
                    src = bass.AP(tensor=cs_dram.tensor, offset=(b * H + j) * S + t * P,
                                  ap=[[0, LC], [2 * S, NG], [1, P]])
                    sp.dma_start(mix[j * LC:(j + 1) * LC, n % 3, :, :], src).then_inc(cs_spread[n % 3], 16)

            def store(n):
                b, t = divmod(n, NT)
                sp.wait_ge(res_ready, n + 1)
                sp.dma_start(out[b, t * P:(t + 1) * P, :], x_sb[:, n, :]).then_inc(stored, 16)

            store_cs(0)
            for n in range(3):
                spread_cs(n)
            store_cs(1)
            for n in range(3, NN):
                spread_cs(n)
                if n >= 5:
                    store(n - 5)
            for n in range(NN - 5, NN):
                store(n)
            sp.wait_ge(stored, 16 * NN)

        @block.gpsimd
        def _(pool):
            pool.memset(ident[:, :], 0.0).then_inc(ident_zero, 1)
            pool.memset(minus_half[:, :], -0.5).then_inc(half_ready, 1)
            pool.memset(tri[:, :], 1.0).then_inc(masks_step, 1)
            pool.memset(suffix[:, :], 1.0).then_inc(masks_step, 1)
            pool.memset(whole[:, :, :], 0.0).then_inc(masks_step, 1)
            pool.wait_ge(ident_zero, 1)
            pool.affine_select(out=ident[:, :], in_=ident[:, :], compare_op=ALU.not_equal, fill=1.0,
                               base=0, pattern=[[-1, P]], channel_multiplier=1).then_inc(ident_ready, 1)
            pool.wait_ge(masks_step, 3)
            pool.affine_select(out=tri[:, :], in_=tri[:, :], compare_op=ALU.is_ge, fill=0.0, base=0,
                               pattern=[[1, P]], channel_multiplier=-1).then_inc(masks_step, 1)
            pool.affine_select(out=suffix[:, :], in_=suffix[:, :], compare_op=ALU.is_ge, fill=0.0, base=-1,
                               pattern=[[-1, P]], channel_multiplier=1).then_inc(masks_step, 1)

            def reciprocal_std(b):
                pool.wait_ge(var_ready, b + 1)
                pool.wait_ge(half_ready, 1)
                pool.tensor_tensor(rstd[:, :], var_eps[:, :], minus_half[:, :], ALU.pow).then_inc(rstd_ready, 1)

            def round_weights(i, nat, q, arrived):
                pool.wait_ge(magic_ready, i + 1)
                pool.wait_ge(arrived, 16)
                pool.tensor_tensor(nat, nat, magic[i % 2], ALU.add).then_inc(added, 1)
                pool.wait_ge(added, i + 1)
                pool.tensor_tensor(q[:, :, :].rearrange("p k i -> p (k i)"), nat, magic[i % 2],
                                   ALU.subtract).then_inc(ffn_q_ready, 1)

            def segments(n):
                b, t = divmod(n, NT)
                pool.wait_ge(cs_spread[n % 3], 32 * (n // 3 + 1))
                pool.wait_ge(cs_s_ready, 4 * (b + 1))
                for part in range(2):
                    gs = slice(part * NG // 2, (part + 1) * NG // 2)
                    seg = mix[:, n % 3, gs, :].rearrange("p g (e l) -> p g e l", l=LC)
                    at_s = cs_s[:, b, gs, 2 * t:2 * t + 2]
                    pool.tensor_tensor(seg, at_s.unsqueeze(3).broadcast_to([P, NG // 2, 2, LC]), seg,
                                       ALU.subtract).then_inc(seg_ready, 1)

            def decayed_x(n):
                b, t = divmod(n, NT)
                pool.wait_ge(decays_ready, 3 * (b + 1))
                pool.wait_ge(xdt_ready, n + 1)
                if n >= 2:
                    wait_states_made(pool, n - 2)
                pool.tensor_tensor(xw[:, n % 2, :].rearrange("p (h q) -> p h q", q=HP),
                                   xdt[:, n % 2, :].rearrange("p (h q) -> p h q", q=HP),
                                   by_head(decay_out[:, b, t, :], [P, H, HP]), ALU.mult).then_inc(xw_ready, 1)

            def fuse_low(k):
                pool.wait_ge(hi_ready, k + 1)
                if k >= 2:
                    pool.wait_ge(down_done, k - 1)
                pool.tensor_tensor(fuse_lo[:, k % 2, :], fuse[:, k % 2, :], fuse_hi[:, k % 2, :].bitcast(F32),
                                   ALU.subtract).then_inc(lo_ready, 1)

            def add_ffn(n):
                pool.wait_ge(ffn_out, n + 1)
                pool.tensor_tensor(x_sb[:, n, :], x_sb[:, n, :], ffn[:, n % 2, :], ALU.add).then_inc(ffn_added, 1)

            def sum_squares(n):
                pool.wait_ge(square_ready, n + 1)
                pool.tensor_tensor(sq2[:, :, :], square[:, 0:2, :], square[:, 2:4, :], ALU.add).then_inc(sq2_ready, 1)
                pool.wait_ge(sq2_ready, n + 1)
                if n:
                    wait_filled(pool, "out", n - 1)
                pool.tensor_tensor(sqsum[:, :], sq2[:, 0, :], sq2[:, 1, :], ALU.add).then_inc(sqsum_ready, 1)

            def reciprocal_rms(n):
                pool.wait_ge(ms_ready, n + 1)
                pool.tensor_tensor(rrms[:, n % 2:n % 2 + 1], ms[:, n % 2:n % 2 + 1], minus_half[:, 0:1],
                                   ALU.pow).then_inc(rrms_ready, 1)

            reciprocal_std(0)
            round_weights(0, gate_nat, gate_q, gate_in)
            round_weights(1, up_nat, up_q, up_in)
            pool.wait_ge(ffn_q_ready, 2)
            pool.memset(xdiag[:, :, :, :], 0.0).then_inc(zeros_ready, 1)
            pool.memset(btok[:, :, :, :], 0.0).then_inc(zeros_ready, 1)
            reciprocal_std(1)
            round_weights(2, down_nat, down_q, down_in)
            for j in range(NP // 2):
                fuse_low(j)
                if j == NI + 1:
                    add_ffn(0)
                    add_ffn(1)
            add_ffn(2)
            add_ffn(3)
            segments(0)
            decayed_x(0)
            for n in range(NN + 1):
                k = NP // 2 + 2 * n
                if k < NP:
                    if n:
                        fuse_low(k - 1)
                elif k == NP:
                    fuse_low(k - 1)
                if n + 1 < NN:
                    segments(n + 1)
                if n:
                    sum_squares(n - 1)
                if k < NP:
                    fuse_low(k)
                if n + 1 < NN:
                    decayed_x(n + 1)
                if n:
                    reciprocal_rms(n - 1)
                if n == 3:
                    add_ffn(4)
                    add_ffn(5)
                if n == 6:
                    add_ffn(6)
                    add_ffn(7)

        @block.tensor
        def _(pe):
            def claim(name, n=0):
                k, before, _ = JOB[name, n]
                if before:
                    pe.wait_ge(*read_out(*before))
                return bank[k]

            def fill(name, n=0):
                return full[JOB[name, n][0]]

            def turn(dst, src, n):
                return pe.transpose(dst, src, ident[0:n, 0:n])

            def turn_w_in(name, arrived, count, blocks):
                pe.wait_ge(arrived, count)
                for k in range(KT):
                    to = claim(f"{name}{k}")
                    for n, r in enumerate(blocks):
                        rows = P if r < 10 else H
                        src = w_nat[:, r, k * P:(k + 1) * P] if r < 10 else w_dt_nat[0:H, k * P:(k + 1) * P]
                        last = turn(to[:, n * P:n * P + rows], src, rows)
                    last.then_inc(fill(f"{name}{k}"), 1)

            def turn_w_out():
                pe.wait_ge(w_out_in, 16)
                for n in range(2):
                    to = claim(f"wo_{n}")
                    for i in range(2):
                        for r in range(2):
                            m = 2 * n + i
                            last = turn(to[:, i * DIM + r * P:i * DIM + (r + 1) * P],
                                        wo_nat[:, r, m * P:(m + 1) * P], P)
                    last.then_inc(fill(f"wo_{n}"), 1)

            def turn_xn(b):
                for k in range(KT):
                    to = claim(f"xn_{k}", b)
                    for t in range(NT):
                        pe.wait_ge(xn_ready, b * NT + t + 1)
                        last = turn(to[:, t * P:(t + 1) * P], xn[:, t, k * P:(k + 1) * P], P)
                    last.then_inc(fill(f"xn_{k}", b), 1)

            def in_projection(name, b, col):
                to = claim(name, b)
                ops = [(w, a, k) for w, a in ((w_hi, xn_hi), (w_lo, xn_hi), (w_hi, xn_lo)) for k in range(KT)]
                for n, (w, a, k) in enumerate(ops):
                    last = pe.matmul(to[:, :], w[:, k, col:col + P], a[:, b, k, :],
                                     start=(n == 0), stop=(n == len(ops) - 1))
                last.then_inc(fill(name, b), 1)

            parts = (da_hi, da_mid, da_lo)

            def sums_of_da(b):
                to = claim("csT", b)
                pe.wait_ge(masks_ready, 7)
                pe.wait_ge(da_split, b + 1)
                for t in range(NT):
                    for n, part in enumerate(parts):
                        last = pe.matmul(to[0:H, t * P:(t + 1) * P], part[:, t, :], tri[:, :],
                                         start=(n == 0), stop=(n == 2))
                last.then_inc(fill("csT", b), 1)
                to = claim("cs", b)
                for t in range(NT):
                    for n, part in enumerate(parts):
                        pe.matmul(to[:, t * H:(t + 1) * H], tri[:, :], part[:, t, :], start=(n == 0), stop=(n == 2))
                for t in range(NT):
                    for n, part in enumerate(parts):
                        pe.matmul(to[:, P + t * H:P + (t + 1) * H], suffix[:, :], part[:, t, :],
                                  start=(n == 0), stop=(n == 2))
                for c in range(NC):
                    for n, part in enumerate(parts):
                        last = pe.matmul(to[:, 2 * P + c * H:2 * P + (c + 1) * H], whole[:, c % 2, :],
                                         part[:, c // 2, :], start=(n == 0), stop=(n == 2))
                last.then_inc(fill("cs", b), 1)

            def turn_dt(b):
                to = claim("dtok", b)
                pe.wait_ge(da_ready, b + 1)
                for t in range(NT):
                    last = pe.transpose(to[:, t * 2 * H:(t + 1) * 2 * H], dtA[2 * H:4 * H, t * P:(t + 1) * P],
                                        ident[2 * H:4 * H, 2 * H:4 * H])
                last.then_inc(fill("dtok", b), 1)

            def gate_up(k):
                h, i = divmod(k, NI)
                b, half = divmod(h, 2)
                if k == 0:
                    pe.wait_ge(ffn_q_ready, 2)
                to = claim("gu", k)
                for at, q in ((0, gate_q), (SH, up_q)):
                    for n, (part, kt) in enumerate([(part, kt) for kt in range(KT) for part in (xn_hi, xn_lo)]):
                        last = pe.matmul(to[:, at:at + SH], q[:, kt, i * P:(i + 1) * P],
                                         part[:, b, kt, half * SH:(half + 1) * SH],
                                         start=(n == 0), stop=(n == 2 * KT - 1))
                last.then_inc(fill("gu", k), 1)

            def down(k):
                h, i = divmod(k, NI)
                to = claim("down", h) if i == 0 else bank_of("down", h)
                if k == 0:
                    pe.wait_ge(ffn_q_ready, 3)
                pe.wait_ge(lo_ready, k + 1)
                for t in range(2):
                    for part in (fuse_hi, fuse_lo):
                        last = pe.matmul(to[:, t * DIM:(t + 1) * DIM], part[:, k % 2, t * P:(t + 1) * P],
                                         down_q[:, i, :], start=(i == 0 and t == 0 and part is fuse_hi),
                                         stop=(i == NI - 1 and part is fuse_lo), skip_group_check=True)
                last.then_inc(down_done, 1)

            def turn_tokens(n):
                b, t = divmod(n, NT)
                cols = slice(t * P, (t + 1) * P)
                to = claim("xtok", n)
                for m in range(NM):
                    last = turn(to[:, m * P:(m + 1) * P], xbc[:, b, m, cols], P)
                last.then_inc(fill("xtok", n), 1)
                to = claim("btcb", n)
                turn(to[:, 0:P], xbc[:, b, 4, cols], P)
                pe.matmul(to[:, P:2 * P], xbc[:, b, 4, cols], xbc[:, b, 5, cols],
                          start=True, stop=True).then_inc(fill("btcb", n), 1)

            def chunk_state(c):
                n, e = divmod(c, 2)
                to = claim("s", c)
                if e == 0:
                    pe.wait_ge(btok_ready, 2 * n + 2)
                    pe.wait_ge(xw_ready, n + 1)
                pe.matmul(to[:, :], btok[:, n % 2, e, :], xw[:, n % 2, :], start=True,
                          stop=True).then_inc(fill("s", c), 1)

            def from_states(n):
                b, t = divmod(n, NT)
                to = claim("inter", n)
                for e in range(2):
                    if t or e:
                        c = 2 * n + e
                        pe.wait_ge(state_ready, states_before(c))
                        at = t * P + e * LC
                        pe.matmul(to[e * LC:(e + 1) * LC, :], xbc[:, b, 5, at:at + LC], state[:, c % 3, :],
                                  start=True, stop=True).then_inc(inter_done, 1)

            def within_chunks(n):
                b, t = divmod(n, NT)
                to = claim("y", n)
                if n == 0:
                    pe.wait_ge(diag_ready, NM)
                for m in range(NM):
                    pe.matmul(to[:, m * P:(m + 1) * P], diag_d[:, m, :], xbc[:, b, m, t * P:(t + 1) * P],
                              start=(m == 0), stop=False, skip_group_check=True)
                pe.wait_ge(xdiag_ready, 4 * n + 4)
                for m in range(NM):
                    if m % 2 == 0:
                        pe.wait_ge(mix_ready, 2 * n + m // 2 + 1)
                    for e in range(2):
                        for i in range(GM):
                            g = m * GM + i
                            at = m * P + e * LC
                            pe.matmul(to[32 * i:32 * (i + 1), at:at + LC],
                                      xdiag[:, n % 2, e, 32 * g:32 * (g + 1)],
                                      mix[:, n % 3, g, e * LC:(e + 1) * LC],
                                      start=False, stop=False, skip_group_check=True)
                pe.wait_ge(inter_ready, n + 1)
                for m in range(NM):
                    last = pe.matmul(to[:, m * P:(m + 1) * P], inter[:, n % 2, m * P:(m + 1) * P], ident[:, :],
                                     start=False, stop=True, skip_group_check=True)
                last.then_inc(fill("y", n), 1)

            def out_projection(n):
                b, t = divmod(n, NT)
                to = claim("out", n)
                if n == 0:
                    pe.wait_ge(wo_ready, NM)
                pe.wait_ge(y_ready, n + 1)
                for m in range(NM):
                    pe.matmul(to[:, 0:DIM], sz[:, b, m, t * P:(t + 1) * P], woT[:, m, :], start=(m == 0),
                              stop=(m == NM - 1), skip_group_check=True)

            def sum_of_squares(n):
                pe.wait_ge(sqsum_ready, n + 1)
                pe.matmul(bank_of("out", n)[:, DIM:DIM + 1], sqsum[:, :], ones[:, :], start=False, stop=True,
                          skip_group_check=True).then_inc(fill("out", n), 1)

            def convolved(n, b):
                i = CONV_ORDER[n]
                in_projection(f"conv_{i}", b, HID + i * P)

            def dt_projection(b):
                in_projection("dt", b, 2 * HID + 2 * NS + H - P)

            pe.wait_ge(ident_ready, 1)
            turn_w_in("w_b", w_b_in, 32, (8, 9, 10))
            turn_xn(0)
            turn_w_in("w_a", w_a_in, 16, range(4, 8))
            pe.wait_ge(w_lo_ready, 2)
            pe.wait_ge(xn_lo_ready, KT)
            dt_projection(0)
            convolved(0, 0)
            convolved(1, 0)
            turn_w_out()
            pe.wait_ge(w_lo_ready, 4)
            convolved(2, 0)
            turn_dt(0)
            convolved(3, 0)
            turn_w_in("w_c", w_c_in, 16, range(0, 4))
            convolved(4, 0)
            convolved(5, 0)
            pe.wait_ge(w_lo_ready, 6)
            for i in range(NM):
                in_projection(f"z_{i}", 0, i * P)
            sums_of_da(0)
            turn_xn(1)
            gate_up(0)
            pe.wait_ge(xn_lo_ready, 2 * KT)
            dt_projection(1)
            for j in range(NP // 2):
                if j < NV:
                    convolved(j, 1)
                elif j < NV + NM:
                    in_projection(f"z_{j - NV}", 1, (j - NV) * P)
                if j == 2:
                    turn_dt(1)
                if j == 4:
                    sums_of_da(1)
                if j + 1 < NP // 2:
                    gate_up(j + 1)
                down(j)
            pe.wait_ge(silu_done, NV)
            turn_tokens(0)
            for n in range(NN):
                k = NP // 2 + 2 * n
                chunk_state(2 * n)
                if n + 1 < NN:
                    if n + 1 == NT:
                        pe.wait_ge(silu_done, 2 * NV)
                    turn_tokens(n + 1)
                if k < NP:
                    gate_up(k)
                if n:
                    out_projection(n - 1)
                if n and k <= NP:
                    down(k - 1)
                if n % NT < NT - 1:
                    chunk_state(2 * n + 1)
                if k < NP:
                    gate_up(k + 1)
                if n:
                    sum_of_squares(n - 1)
                if k < NP:
                    down(k)
                from_states(n)
                within_chunks(n)
            out_projection(NN - 1)
            sum_of_squares(NN - 1)

        @block.scalar
        def _(act):
            with nc.allow_non_contiguous_dma(reason="small parameters"):
                act.dma_start(heads[3 * H:4 * H, 0:1],
                              dt_bias.rearrange("(h o) -> h o", o=1)).then_inc(front_params_in, 16)
                act.dma_start(heads[3 * H:4 * H, 1:2],
                              a_log.rearrange("(h o) -> h o", o=1)).then_inc(front_params_in, 16)
                act.dma_start(convw[:, :, :], conv_w.rearrange("(m p) k -> p m k", p=P)).then_inc(front_params_in, 16)
                act.dma_start(convb[:, :], conv_b.rearrange("(m p) -> p m", p=P)).then_inc(front_params_in, 16)
                act.dma_start(normw[:, :], norm_w.rearrange("(m p) -> p m", p=P)).then_inc(norm_w_in, 16)

            def weights_high(name, col, width):
                for k in range(KT):
                    src = wait_filled(act, f"{name}{k}")
                    act.activation(w_hi[:, k, col:col + width], src[:, 0:width], ACT.Copy).then_inc(w_hi_ready, 1)

            def xn_high(b):
                for k in range(KT):
                    src = wait_filled(act, f"xn_{k}", b)
                    act.activation(xn_hi[:, b, k, :], src[:, :], ACT.Copy).then_inc(xn_hi_ready, 1)

            def softplus(b):
                src = wait_filled(act, "dt", b)
                if b:
                    wait_filled(act, "dtok", b - 1)
                act.activation(dtA[3 * H:4 * H, :], src[3 * H:4 * H, :], ACT.Exp,
                               bias=heads[3 * H:4 * H, 0:1]).then_inc(dt_exp, 1)
                act.wait_ge(dt_exp, b + 1)
                act.activation(dtA[3 * H:4 * H, :], dtA[3 * H:4 * H, :], ACT.Ln, bias=1.0).then_inc(dt_ln, 1)

            def last_tap(n, b):
                i = CONV_ORDER[n]
                src = wait_filled(act, f"conv_{i}", b)
                act.activation(xbc[:, b, i, :], src[:, :], ACT.Identity, bias=convb[:, i:i + 1],
                               scale=convw[:, i, TAPS - 1:TAPS]).then_inc(tap_done, 1)

            def w_out_normed():
                act.wait_ge(norm_w_in, 16)
                for m in range(NM):
                    src = wait_filled(act, f"wo_{m // 2}")
                    act.activation(woT[:, m, :], src[:, (m % 2) * DIM:(m % 2 + 1) * DIM], ACT.Copy,
                                   scale=normw[:, m:m + 1]).then_inc(wo_ready, 1)

            def diagonals():
                act.wait_ge(d_skip_in, 16 * NM)
                for m in range(NM):
                    act.activation(diag_d[:, m, :], ident[:, :], ACT.Copy, scale=dcol[:, m:m + 1]).then_inc(diag_ready, 1)

            def decays(b):
                src = wait_filled(act, "csT", b)
                if b:
                    act.wait_ge(cs_stored, 16 * b)
                act.activation(csT[:, :], src[0:H, :], ACT.Copy).then_inc(csT_ready, 1)
                src = wait_filled(act, "cs", b)
                act.activation(decay_in[:, b, :, :], src[:, 0:P].rearrange("p (t h) -> p t h", h=H),
                               ACT.Exp).then_inc(decays_ready, 1)
                act.activation(decay_out[:, b, :, :], src[:, P:2 * P].rearrange("p (t h) -> p t h", h=H),
                               ACT.Exp).then_inc(decays_ready, 1)
                act.activation(decay_all[:, b, :, :], src[:, 2 * P:4 * P].rearrange("p (c h) -> p c h", h=H),
                               ACT.Exp).then_inc(decays_ready, 1)

            def silu_conv(n, b):
                i = CONV_ORDER[n]
                act.wait_ge(conv_done, b * NV + n + 1)
                act.activation(xbc[:, b, i, :], xbc[:, b, i, :], ACT.Silu).then_inc(silu_done, 1)

            def silu_z(i, b):
                src = wait_filled(act, f"z_{i}", b)
                act.activation(sz[:, b, i, :], src[:, :], ACT.Silu).then_inc(sz_ready, 1)

            def gate(k):
                i = k % NI
                src = wait_filled(act, "gu", k)
                if k >= 2:
                    act.wait_ge(lo_ready, k - 1)
                act.activation(fuse[:, k % 2, :], src[:, 0:SH], ACT.Silu,
                               scale=gscale[:, i:i + 1]).then_inc(gate_ready, 1)

            def fuse_high(k):
                act.wait_ge(fuse_ready, k + 1)
                if k >= 2:
                    act.wait_ge(down_done, k - 1)
                act.activation(fuse_hi[:, k % 2, :], fuse[:, k % 2, :], ACT.Copy).then_inc(hi_ready, 1)

            def b_tokens(n):
                src = wait_filled(act, "btcb", n)
                act.wait_ge(zeros_ready, 2)
                if n >= 2:
                    wait_states_made(act, n - 2)
                for e in range(2):
                    rows = slice(e * LC, (e + 1) * LC)
                    act.activation(btok[rows, n % 2, e, :], src[rows, 0:P], ACT.Copy).then_inc(btok_ready, 1)

            def spread_x(n):
                act.wait_ge(xdt_ready, n + 1)
                act.wait_ge(zeros_ready, 2)
                if n >= 2:
                    wait_filled(act, "y", n - 2)
                pick = lambda ap: ap.rearrange("p (g j q) -> p g j q", j=2, q=HP)
                for e in range(2):
                    for j in range(2):
                        act.activation(pick(xdiag[j * LC:(j + 1) * LC, n % 2, e, :])[:, :, j, :],
                                       pick(xdt[e * LC:(e + 1) * LC, n % 2, :])[:, :, j, :],
                                       ACT.Copy).then_inc(xdiag_ready, 1)

            def exp_segments(n):
                for part in range(2):
                    seg = mix[:, n % 3, part * NG // 2:(part + 1) * NG // 2, :]
                    act.wait_ge(seg_ready, 2 * n + part + 1)
                    act.activation(seg, seg, ACT.Relu).then_inc(seg_capped, 1)
                    act.wait_ge(seg_capped, 2 * n + part + 1)
                    act.activation(seg, seg, ACT.Exp, scale=-1.0).then_inc(seg_exp, 1)

            def squares(n):
                b, t = divmod(n, NT)
                act.wait_ge(y_ready, n + 1)
                if n:
                    act.wait_ge(sq2_ready, n)
                act.activation(square[:, :, :], sz[:, b, :, t * P:(t + 1) * P], ACT.Square).then_inc(square_ready, 1)

            weights_high("w_b", HID + 512, 2 * P + H)
            xn_high(0)
            act.wait_ge(front_params_in, 4 * 16)
            act.activation(heads[3 * H:4 * H, 2:3], heads[3 * H:4 * H, 1:2], ACT.Exp).then_inc(a_exp, 1)
            weights_high("w_a", HID, 512)
            softplus(0)
            last_tap(0, 0)
            last_tap(1, 0)
            w_out_normed()
            last_tap(2, 0)
            last_tap(3, 0)
            weights_high("w_c", 0, 512)
            last_tap(4, 0)
            last_tap(5, 0)
            for n in range(NM):
                silu_conv(n, 0)
            for i in range(NM):
                silu_z(i, 0)
            for n in range(NM, NV):
                silu_conv(n, 0)
            decays(0)
            xn_high(1)
            diagonals()
            softplus(1)
            act.wait_ge(scales_in, 3 * 16)
            gate(0)
            act.wait_ge(ffn_q_ready, 3)
            for j in range(NP // 2):
                fuse_high(j)
                if j < NV:
                    last_tap(j, 1)
                elif j < NV + NM:
                    silu_conv(j - NV, 1)
                    silu_z(j - NV, 1)
                if j == NV - 1:
                    decays(1)
                if j + 1 < NP // 2:
                    gate(j + 1)
            for n in range(NM, NV):
                silu_conv(n, 1)
            b_tokens(0)
            spread_x(0)
            exp_segments(0)
            for n in range(NN):
                k = NP // 2 + 2 * n
                if k < NP:
                    gate(k)
                if n + 1 < NN:
                    b_tokens(n + 1)
                if k < NP:
                    fuse_high(k)
                if n:
                    squares(n - 1)
                if k < NP:
                    gate(k + 1)
                if n + 1 < NN:
                    spread_x(n + 1)
                if k < NP:
                    fuse_high(k + 1)
                if n + 1 < NN:
                    exp_segments(n + 1)
            squares(NN - 1)

        @block.vector
        def _(dve):
            def masks():
                dve.wait_ge(masks_step, 5)
                dve.memset(whole[0:LC, 0, :], 1.0).then_inc(masks_ready, 1)
                dve.memset(whole[LC:P, 1, :], 1.0).then_inc(masks_ready, 1)
                dve.memset(tri[0:LC, LC:P], 0.0).then_inc(masks_ready, 1)
                dve.memset(suffix[LC:P, 0:LC], 0.0).then_inc(masks_ready, 1)
                for e in range(2):
                    dve.tensor_copy(causal[e * LC:(e + 1) * LC, :],
                                    tri[e * LC:(e + 1) * LC, e * LC:(e + 1) * LC]).then_inc(masks_ready, 1)
                dve.memset(ones[:, :], 1.0).then_inc(masks_ready, 1)

            def layer_norm_stats(b):
                for t in range(NT):
                    if t % 2 == 0:
                        dve.wait_ge(x_in[2 * b + t // 2], 16)
                    if b and t == 0:
                        dve.wait_ge(xn_ready, NT * b)
                    dve.bn_stats(stats[:, t, :], x_sb[:, b * NT + t, :]).then_inc(stats_done, 1)
                for t in range(NT):
                    dve.wait_ge(stats_done, b * NT + t + 1)
                    dve.bn_aggr(meanvar[:, t, :], stats[:, t, :]).then_inc(meanvar_done, 1)
                dve.wait_ge(meanvar_done, NT * (b + 1))
                dve.tensor_scalar(var_eps[:, :], meanvar[:, :, 1], LN_EPS, None, ALU.add).then_inc(var_ready, 1)

            def layer_norm(b):
                dve.wait_ge(rstd_ready, b + 1)
                if b:
                    wait_filled(dve, "xn_1", b - 1)
                for t in range(NT):
                    dve.tensor_scalar(xn[:, t, :], x_sb[:, b * NT + t, :], meanvar[:, t, 0:1], rstd[:, t:t + 1],
                                      ALU.subtract, ALU.mult).then_inc(xn_ready, 1)

            def weights_low(name, n, col, width):
                for k in range(KT):
                    src = wait_filled(dve, f"{name}{k}")
                    dve.wait_ge(w_hi_ready, n + k + 1)
                    dve.tensor_tensor(w_lo[:, k, col:col + width], src[:, 0:width],
                                      w_hi[:, k, col:col + width].bitcast(F32),
                                      ALU.subtract).then_inc(w_lo_ready, 1)

            def magic_numbers(i, nat, arrived):
                dve.wait_ge(arrived, 16)
                if i >= 2:
                    dve.wait_ge(ffn_q_ready, i - 1)
                dve.tensor_scalar(magic[i % 2].bitcast(U32), nat.bitcast(U32), EXPONENT, None,
                                  ALU.bitwise_and).then_inc(expo_step, 1)
                dve.wait_ge(expo_step, i + 1)
                dve.tensor_scalar(magic[i % 2], magic[i % 2], E4M3_MIN_NORMAL, ROUND_TO_E4M3, ALU.max,
                                  ALU.mult).then_inc(magic_ready, 1)

            def xn_low(b):
                for k in range(KT):
                    src = wait_filled(dve, f"xn_{k}", b)
                    dve.wait_ge(xn_hi_ready, b * KT + k + 1)
                    dve.tensor_tensor(xn_lo[:, b, k, :], src[:, :], xn_hi[:, b, k, :].bitcast(F32),
                                      ALU.subtract).then_inc(xn_lo_ready, 1)

            def time_steps(b):
                dve.wait_ge(dt_ln, b + 1)
                dt = dtA[3 * H:4 * H, :]
                dve.tensor_scalar(dt, dt, DT_MIN, DT_MAX, ALU.max, ALU.min).then_inc(dt_clipped, 1)
                dve.wait_ge(dt_clipped, b + 1)
                dve.tensor_scalar(dtA[2 * H:3 * H, :], dt, heads[3 * H:4 * H, 3:4], None,
                                  ALU.mult).then_inc(da_ready, 1)

            def other_taps(n, b):
                i = CONV_ORDER[n]
                src = bank_of(f"conv_{i}", b)
                dve.wait_ge(tap_done, b * NV + n + 1)
                for k in range(1, TAPS):
                    if k > 1:
                        dve.wait_ge(tap_step, (b * NV + n) * (TAPS - 2) + k - 1)
                    done = tap_step if k < TAPS - 1 else conv_done
                    dve.scalar_tensor_tensor(out=xbc[:, b, i, k:S], in0=src[:, 0:S - k],
                                             scalar=convw[:, i, TAPS - 1 - k:TAPS - k], in1=xbc[:, b, i, k:S],
                                             op0=ALU.mult, op1=ALU.add).then_inc(done, 1)

            def split_da(b):
                src = wait_filled(dve, "dtok", b)[:, 0:NT * 2 * H].rearrange("p (t h) -> p t h", h=2 * H)
                if b:
                    wait_filled(dve, "cs", b - 1)
                da = src[:, :, 0:H]
                dve.tensor_copy(dtok[:, b, :, :], src[:, :, H:2 * H]).then_inc(dtok_ready, 1)
                dve.tensor_copy(da_hi[:, :, :], da).then_inc(dtok_step, 1)
                dve.wait_ge(dtok_step, 3 * b + 1)
                dve.tensor_tensor(rest1[:, :, :], da, da_hi[:, :, :], ALU.subtract).then_inc(dtok_step, 1)
                dve.wait_ge(dtok_step, 3 * b + 2)
                dve.tensor_copy(da_mid[:, :, :], rest1[:, :, :]).then_inc(dtok_step, 1)
                dve.wait_ge(dtok_step, 3 * b + 3)
                dve.tensor_tensor(da_lo[:, :, :], rest1[:, :, :], da_mid[:, :, :], ALU.subtract).then_inc(da_split, 1)

            def chunk_sums(b):
                src = bank_of("cs", b)
                dve.wait_ge(decays_ready, 3 * (b + 1))
                for j in range(2):
                    for e in range(2):
                        rows = slice(e * LC, (e + 1) * LC)
                        pick = lambda ap: ap.rearrange("p t (g j) -> p t g j", j=2)[:, :, :, j]
                        dve.tensor_copy(
                            cs_s[j * LC:(j + 1) * LC, b, :, e:NC:2].rearrange("p g t -> p t g"),
                            pick(src[rows, 0:P].rearrange("p (t h) -> p t h", t=NT))).then_inc(cs_s_ready, 1)

            def x_times_dt(n):
                b, t = divmod(n, NT)
                src = wait_filled(dve, "xtok", n)
                dve.wait_ge(dtok_ready, b + 1)
                if n >= 2:
                    dve.wait_ge(xdiag_ready, 4 * n - 4)
                    dve.wait_ge(xw_ready, n - 1)
                dve.tensor_tensor(xdt[:, n % 2, :].rearrange("p (h q) -> p h q", q=HP),
                                  src[:, :].rearrange("p (h q) -> p h q", q=HP),
                                  by_head(dtok[:, b, t, :], [P, H, HP]), ALU.mult).then_inc(xdt_ready, 1)

            def masked_cb(n):
                dve.wait_ge(masks_ready, 7)
                dve.wait_ge(btok_ready, 2 * n + 2)
                src = bank_of("btcb", n)
                for e in range(2):
                    rows = slice(e * LC, (e + 1) * LC)
                    for j in range(2):
                        dve.tensor_tensor(cbm[j * LC:(j + 1) * LC, n % 2, e, :],
                                          src[rows, P + e * LC:P + (e + 1) * LC], causal[rows, :],
                                          ALU.mult).then_inc(cbm_ready, 1)

            def next_state(c):
                first = c % NC == 0
                b = c // NC
                src = wait_filled(dve, "s", c)
                new = state[:, (c + 1) % 3, :]
                n = states_before(c)
                if n >= 3:
                    dve.wait_ge(inter_done, n - 2)
                if first:
                    dve.tensor_copy(new, src[:, :]).then_inc(state_ready, 1)
                else:
                    dve.wait_ge(state_ready, n)
                    dve.tensor_tensor(new.rearrange("p (h q) -> p h q", q=HP),
                                      state[:, c % 3, :].rearrange("p (h q) -> p h q", q=HP),
                                      by_head(decay_all[:, b, c % NC, :], [P, H, HP]), ALU.mult).then_inc(state_scaled, 1)
                    dve.wait_ge(state_scaled, n - b)
                    dve.tensor_tensor(new, new, src[:, :], ALU.add).then_inc(state_ready, 1)

            def scale_inter(n):
                b, t = divmod(n, NT)
                if n >= 2:
                    wait_filled(dve, "y", n - 2)
                if t == 0:
                    dve.memset(inter[0:LC, n % 2, :], 0.0).then_inc(inter_zero, 1)
                    dve.wait_ge(inter_zero, b + 1)
                dve.wait_ge(inter_done, states_before(2 * n + 1))
                rows = slice(LC if t == 0 else 0, P)
                count = P - rows.start
                src = bank_of("inter", n)
                dve.tensor_tensor(inter[rows, n % 2, :].rearrange("p (h q) -> p h q", q=HP),
                                  src[rows, :].rearrange("p (h q) -> p h q", q=HP),
                                  by_head(decay_in[rows, b, t, :], [count, H, HP]), ALU.mult).then_inc(inter_ready, 1)

            def fuse_up(k):
                src = bank_of("gu", k)
                dve.wait_ge(gate_ready, k + 1)
                dve.scalar_tensor_tensor(out=fuse[:, k % 2, :], in0=src[:, SH:2 * SH], scalar=uscale[:, k % NI:k % NI + 1],
                                         in1=fuse[:, k % 2, :], op0=ALU.mult, op1=ALU.mult).then_inc(fuse_ready, 1)

            def mix_tile(n, part):
                if part == 0:
                    dve.wait_ge(cbm_ready, 4 * n + 4)
                dve.wait_ge(seg_exp, 2 * n + part + 1)
                seg = mix[:, n % 3, part * NG // 2:(part + 1) * NG // 2, :]
                cb = cbm[:, n % 2, :, :].rearrange("p e l -> p (e l)")
                dve.tensor_tensor(seg, seg, cb.unsqueeze(1).broadcast_to([P, NG // 2, P]),
                                  ALU.mult).then_inc(mix_ready, 1)

            def gated(n):
                b, t = divmod(n, NT)
                cols = slice(t * P, (t + 1) * P)
                src = wait_filled(dve, "y", n)
                dve.wait_ge(sz_ready, NM * (b + 1))
                dve.tensor_tensor(sz[:, b, :, cols], src[:, :].rearrange("p (m l) -> p m l", m=NM), sz[:, b, :, cols],
                                  ALU.mult).then_inc(y_ready, 1)

            def ffn_result(h):
                src = wait_filled_down(h)
                for t in range(2):
                    n = 2 * h + t
                    if n >= 2:
                        dve.wait_ge(ffn_added, n - 1)
                    dve.tensor_tensor(ffn[:, n % 2, :], src[:, t * DIM:(t + 1) * DIM], dscale[:, :],
                                      ALU.mult).then_inc(ffn_out, 1)

            def wait_filled_down(h):
                dve.wait_ge(down_done, NI * (h + 1))
                return bank_of("down", h)

            def mean_square(n):
                src = wait_filled(dve, "out", n)
                if n >= 2:
                    dve.wait_ge(rrms_ready, n - 1)
                dve.tensor_scalar(ms[:, n % 2:n % 2 + 1], src[:, DIM:DIM + 1], 1.0 / HID, RMS_EPS, ALU.mult,
                                  ALU.add).then_inc(ms_ready, 1)

            def result(n):
                dve.wait_ge(rrms_ready, n + 1)
                dve.wait_ge(ffn_added, n + 1)
                src = bank_of("out", n)
                dve.scalar_tensor_tensor(out=x_sb[:, n, :], in0=src[:, 0:DIM], scalar=rrms[:, n % 2:n % 2 + 1],
                                         in1=x_sb[:, n, :], op0=ALU.mult, op1=ALU.add).then_inc(res_ready, 1)

            layer_norm_stats(0)
            layer_norm(0)
            masks()
            weights_low("w_b", 0, HID + 512, 2 * P + H)
            xn_low(0)
            dve.wait_ge(a_exp, 1)
            dve.tensor_scalar(heads[3 * H:4 * H, 3:4], heads[3 * H:4 * H, 2:3], -1.0, None,
                              ALU.mult).then_inc(a_neg, 1)
            weights_low("w_a", 2, HID, 512)
            magic_numbers(0, gate_nat, gate_in)
            dve.wait_ge(a_neg, 1)
            time_steps(0)
            other_taps(0, 0)
            magic_numbers(1, up_nat, up_in)
            other_taps(1, 0)
            weights_low("w_c", 4, 0, 512)
            other_taps(2, 0)
            magic_numbers(2, down_nat, down_in)
            layer_norm_stats(1)
            other_taps(3, 0)
            split_da(0)
            layer_norm(1)
            other_taps(4, 0)
            other_taps(5, 0)
            chunk_sums(0)
            xn_low(1)
            dve.wait_ge(scales_in, 3 * 16)
            fuse_up(0)
            time_steps(1)
            for j in range(NP // 2):
                if j < NV:
                    other_taps(j, 1)
                if j == 2:
                    split_da(1)
                if j == NV:
                    chunk_sums(1)
                    ffn_result(0)
                if j + 1 < NP // 2:
                    fuse_up(j + 1)
            ffn_result(1)
            x_times_dt(0)
            masked_cb(0)
            mix_tile(0, 0)
            for n in range(NN):
                k = NP // 2 + 2 * n
                if n:
                    gated(n - 1)
                mix_tile(n, 1)
                next_state(2 * n)
                if k < NP:
                    fuse_up(k)
                if n + 1 < NN:
                    x_times_dt(n + 1)
                    masked_cb(n + 1)
                if n % NT < NT - 1:
                    next_state(2 * n + 1)
                if n == 3:
                    ffn_result(2)
                if n == 6:
                    ffn_result(3)
                if k < NP:
                    fuse_up(k + 1)
                scale_inter(n)
                if n:
                    mean_square(n - 1)
                    result(n - 1)
                if n + 1 < NN:
                    mix_tile(n + 1, 0)
            gated(NN - 1)
            mean_square(NN - 1)
            result(NN - 1)


_INS = ['L0_attn_x', 'L0_attn_W_in', 'L0_attn_conv_w', 'L0_attn_conv_b', 'L0_attn_dt_bias', 'L0_attn_A_log',
        'L0_attn_D', 'L0_attn_norm_w', 'L0_attn_W_out', 'L0_ffn_gate_w', 'L0_ffn_up_w', 'L0_ffn_down_w',
        'L0_ffn_gate_scale', 'L0_ffn_up_scale', 'L0_ffn_down_scale']


def kernel(**inputs):
    import numpy as _np
    import concourse.bacc as _bacc
    from concourse import mybir as _mybir
    from concourse.bass_utils import run_bass_kernel_spmd as _run

    nc = _bacc.Bacc("TRN2", target_bir_lowering=False, num_devices=1)
    arrays, args = {}, []
    for name in _INS:
        a = _np.ascontiguousarray(inputs[name])
        arrays[f"in_{name}"] = a
        args.append(nc.dram_tensor(f"in_{name}", a.shape, _mybir.dt.from_np(a.dtype), kind="ExternalInput").ap())
    shape = inputs['L0_attn_x'].shape
    args.append(nc.dram_tensor("out_0", shape, _mybir.dt.float32, kind="ExternalOutput").ap())
    mamba_and_ffn_block(nc, *args)
    r = _run(nc, [arrays], core_ids=[0])
    return r.results[0]["out_0"]
```

```python
from contextlib import ExitStack

import concourse.bass as bass
from concourse import mybir

ALU = mybir.AluOpType
ACT = mybir.ActivationFunctionType
F32 = mybir.dt.float32
F32R = mybir.dt.float32r
BF16 = mybir.dt.bfloat16
U32 = mybir.dt.uint32

P = 128
LC = 64
NS = 128
HP = 16
LN_EPS = 1e-5
RMS_EPS = 1e-6
DT_MIN, DT_MAX = 0.001, 0.1
EXPONENT = 0x7F800000
E4M3_MIN_NORMAL = 2.0 ** -6
ROUND_TO_E4M3 = 1.5 * 2.0 ** 20

CONV_ORDER = (4, 5, 0, 1, 2, 3)

BANKS = [
    [("xn_0", 0), ("w_c0", 0), ("conv_3", 0), ("dtok", 1)] + [("xtok", n) for n in range(8)]
    + [("squares", 7)],
    [("xn_1", 0), ("w_c1", 0), ("csT", 0), ("z_1", 0)] + [("btcb", n) for n in range(8)],
    [("w_b0", 0), ("dt", 0), ("dtok", 0), ("cs", 0), ("z_2", 0)] + [("gu", k) for k in range(3, 14, 2)]
    + [("s", c) for c in range(1, 16) if c % 8 != 7],
    [("w_b1", 0), ("conv_4", 0), ("xn_0", 1), ("z_0", 0), ("gu", 1), ("conv_5", 1), ("conv_2", 1), ("z_1", 1), ("s", 0)]
    + [("inter", n) for n in range(8)],
    [("w_a0", 0), ("conv_5", 0), ("xn_1", 1), ("dt", 1), ("z_3", 0), ("conv_0", 1), ("conv_3", 1), ("z_2", 1), ("cs", 1)]
    + [("y", n) for n in range(8)],
    [("w_a1", 0), ("conv_0", 0), ("conv_4", 1), ("conv_1", 1), ("z_0", 1), ("z_3", 1), ("csT", 1)]
    + [("out", n) for n in range(8)],
    [("wo_0", 0), ("conv_1", 0)] + [("gu", k) for k in range(0, 14, 2)] + [("gu", k) for k in range(14, 24)],
    [("wo_1", 0), ("conv_2", 0)] + [("down", h) for h in range(4)],
]


def number_jobs():
    found = {}
    for k, users in enumerate(BANKS):
        before, fills = None, 0
        for job in users:
            fills += job[0] not in ("inter", "down")
            found[job] = k, before, fills
            before = job
    return found


def mamba_and_ffn_block(nc, x, w_in, conv_w, conv_b, dt_bias, a_log, d_skip, norm_w, w_out,
                        gate_w, up_w, down_w, gate_scale, up_scale, down_scale, out):
    NB, S, DIM = x.shape
    H = a_log.shape[0]
    HID = norm_w.shape[0]
    CONV = conv_w.shape[0]
    I = gate_w.shape[1]
    TAPS = conv_w.shape[1]
    NT = S // P
    NN = NB * NT
    NC = S // LC
    KT = DIM // P
    NM = HID // P
    NV = CONV // P
    NI = I // P
    NG = H // 2
    GM = NG // NM
    SH = S // 2
    NP = NI * 2 * NB
    Z_STEPS = (4, 5, 6, 7)
    BY_TANH = NP // 2
    JOB = number_jobs()

    with ExitStack() as ctx:
        def sb(name, shape, dt=F32):
            return ctx.enter_context(nc.sbuf_tensor(name, shape, dt))

        def sem(name):
            return ctx.enter_context(nc.semaphore(name))

        bank = [ctx.enter_context(nc.psum_tensor(f"bank{i}", [P, 512], F32)) for i in range(8)]
        cs_dram = nc.dram_tensor("cs_scratch", [NB, H, S], F32).ap()

        ident = sb("ident", [P, P])
        tri = sb("tri", [P, P], BF16)
        suffix = sb("suffix", [P, P], BF16)
        whole = sb("whole", [P, 2, P], BF16)
        causal = sb("causal", [P, LC])
        ones = sb("ones", [P, 1])
        minus_half = sb("minus_half", [P, NT])
        convw = sb("convw", [P, NV, TAPS])
        convb = sb("convb", [P, NV])
        heads = sb("heads", [P, 4])
        dcol = sb("dcol", [P, NM])
        normw = sb("normw", [P, NM])
        gscale = sb("gscale", [P, NI])
        uscale = sb("uscale", [P, NI])
        dscale = sb("dscale", [P, DIM])
        half_gscale = sb("half_gscale", [P, NI])
        guscale = sb("guscale", [P, NI])
        w_hi = sb("w_hi", [P, KT, 2 * HID + 2 * NS + H], F32R)
        w_lo = sb("w_lo", [P, KT, 2 * HID + 2 * NS + H], F32R)
        woT = sb("woT", [P, NM, DIM])
        diag_d = sb("diag_d", [P, NM, P])
        gate_q = sb("gate_q", [P, KT, I], F32R)
        up_q = sb("up_q", [P, KT, I], F32R)
        down_q = sb("down_q", [P, NI, DIM], F32R)
        x_sb = sb("x_sb", [P, NN, DIM])
        stats = sb("stats", [P, NT, 6])
        meanvar = sb("meanvar", [P, NT, 2])
        var_eps = sb("var_eps", [P, NT])
        rstd = sb("rstd", [P, NT])
        shift = sb("shift", [P, NT])
        xn = sb("xn", [P, NT, DIM])
        xn_hi = sb("xn_hi", [P, NB, KT, S], F32R)
        xn_lo = sb("xn_lo", [P, NB, KT, S], F32R)
        xbc = sb("xbc", [P, NB, NV, S])
        sz = sb("sz", [P, NB, NM, S])
        dtA = sb("dtA", [P, S])
        csT = sb("csT", [H, S])
        dtok = sb("dtok", [P, NB, NT, H])
        rest1 = sb("rest1", [P, NT, H])
        da_hi = sb("da_hi", [P, NT, H], BF16)
        da_mid = sb("da_mid", [P, NT, H], BF16)
        da_lo = sb("da_lo", [P, NT, H], BF16)
        cs_s = sb("cs_s", [P, NB, NG, NC])
        decay_in = sb("decay_in", [P, NB, NT, H])
        decay_out = sb("decay_out", [P, NB, NT, H])
        decay_all = sb("decay_all", [P, NB, NC, H])
        cbm = sb("cbm", [P, 2, 2, LC])
        mix = sb("mix", [P, 3, NG, P])
        xdiag = sb("xdiag", [P, 2, 2, HID])
        xdt = sb("xdt", [P, 2, HID])
        xw = sb("xw", [P, 2, HID])
        btok = sb("btok", [P, 2, 2, NS])
        state = sb("state", [P, 3, HID])
        inter = sb("inter", [P, 2, HID])
        square = sb("square", [P, NM, P])
        sq2 = sb("sq2", [P, 2, P])
        sqsum = sb("sqsum", [P, P])
        ms = sb("ms", [P, 2])
        rrms = sb("rrms", [P, 2])
        fuse = sb("fuse", [P, 3, SH])
        fuse_hi = sb("fuse_hi", [P, 3, SH], F32R)
        fuse_lo = sb("fuse_lo", [P, 3, SH], F32R)
        ffn = sb("ffn", [P, 2, DIM])

        mix_flat = mix[:, :, :, :].rearrange("p n g t -> p (n g t)")
        w_nat = mix_flat[:, 0:10 * DIM].rearrange("p (r k) -> p r k", k=DIM)
        w_dt_nat = mix_flat[:, 10 * DIM:11 * DIM]
        wo_nat = mix_flat[:, 11 * DIM:11 * DIM + 2 * HID].rearrange("p (r k) -> p r k", k=HID)
        magic = [mix_flat[:, 11 * DIM + 2 * HID:11 * DIM + 2 * HID + KT * I],
                 xdiag[:, :, :, :].rearrange("p n e q -> p (n e q)")[:, 0:KT * I]]
        xbc_flat = xbc[:, 1, :, :].rearrange("p v t -> p (v t)")
        gate_nat = xbc_flat[:, 0:KT * I]
        up_nat = xbc_flat[:, KT * I:2 * KT * I]
        down_nat = sz[:, 1, :, :].rearrange("p m t -> p (m t)")[:, 0:KT * I]

        full = [sem(f"bank{i}_full") for i in range(8)]
        x_in = [sem(f"x_in{h}") for h in range(NN // 2)]
        w_a_in, w_b_in, w_c_in, w_out_in = sem("w_a_in"), sem("w_b_in"), sem("w_c_in"), sem("w_out_in")
        gate_in, up_in, down_in = sem("gate_in"), sem("up_in"), sem("down_in")
        front_params_in, norm_w_in, d_skip_in, scales_in = (
            sem(n) for n in ("front_params_in", "norm_w_in", "d_skip_in", "scales_in"))
        ident_zero, ident_ready = sem("ident_zero"), sem("ident_ready")
        masks_step, masks_ready = sem("masks_step"), sem("masks_ready")
        zeros_ready, half_ready = sem("zeros_ready"), sem("half_ready")
        stats_done, meanvar_done, var_ready, rstd_ready, xn_ready = (
            sem(n) for n in ("stats_done", "meanvar_done", "var_ready", "rstd_ready", "xn_ready"))
        shift_ready = sem("shift_ready")
        w_hi_ready, w_lo_ready, wo_ready = sem("w_hi_ready"), sem("w_lo_ready"), sem("wo_ready")
        expo_step, magic_ready, added, ffn_q_ready = (
            sem("expo_step"), sem("magic_ready"), sem("added"), sem("ffn_q_ready"))
        xn_hi_ready, xn_lo_ready = sem("xn_hi_ready"), sem("xn_lo_ready")
        dt_exp, dt_ln, dt_clipped, da_ready = sem("dt_exp"), sem("dt_ln"), sem("dt_clipped"), sem("da_ready")
        a_exp, a_neg = sem("a_exp"), sem("a_neg")
        dtok_ready, dtok_step, da_split = sem("dtok_ready"), sem("dtok_step"), sem("da_split")
        csT_ready, cs_stored, decays_ready, cs_s_ready = (
            sem(n) for n in ("csT_ready", "cs_stored", "decays_ready", "cs_s_ready"))
        cs_spread = [sem(f"cs_spread{i}") for i in range(3)]
        tap_done, tap_step, conv_done, silu_done, sz_ready = (
            sem(n) for n in ("tap_done", "tap_step", "conv_done", "silu_done", "sz_ready"))
        cbm_ready, xdt_ready, xdiag_ready, xw_ready, btok_ready, diag_ready = (
            sem(n) for n in ("cbm_ready", "xdt_ready", "xdiag_ready", "xw_ready", "btok_ready", "diag_ready"))
        state_scaled, state_ready, inter_done, inter_zero, inter_ready = (
            sem(n) for n in ("state_scaled", "state_ready", "inter_done", "inter_zero", "inter_ready"))
        seg_ready, seg_capped, seg_exp, mix_ready = (
            sem("seg_ready"), sem("seg_capped"), sem("seg_exp"), sem("mix_ready"))
        half_scales_ready, scales_ready, tanh_applied = (
            sem(n) for n in ("half_scales_ready", "scales_ready", "tanh_applied"))
        gate_ready, fuse_ready, hi_ready, lo_ready, down_done = (
            sem(n) for n in ("gate_ready", "fuse_ready", "hi_ready", "lo_ready", "down_done"))
        y_ready, square_ready, sq2_ready, sqsum_ready = (
            sem(n) for n in ("y_ready", "square_ready", "sq2_ready", "sqsum_ready"))
        ms_ready, rrms_ready, ffn_out, ffn_added, res_ready, stored = (
            sem(n) for n in ("ms_ready", "rrms_ready", "ffn_out", "ffn_added", "res_ready", "stored"))

        def wait_filled(eng, name, n=0):
            k, _, fills = JOB[name, n]
            eng.wait_ge(full[k], fills)
            return bank[k]

        def bank_of(name, n=0):
            return bank[JOB[name, n][0]]

        def states_before(c):
            return c - c // NC

        def wait_states_made(eng, n):
            c = 2 * n + 1 if (2 * n + 1) % NC != NC - 1 else 2 * n
            eng.wait_ge(state_ready, states_before(c) + 1)

        def by_head(ap, shape):
            return ap.unsqueeze(2).broadcast_to(shape)

        def read_out(name, n):
            kind, _, i = name.rpartition("_")
            i = int(i) if i.isdigit() else 0
            return {
                "w": lambda: (w_lo_ready, 1 + ("b0", "b1", "a0", "a1", "c0", "c1").index(name[2:])),
                "wo": lambda: (wo_ready, 2 * i + 2),
                "xn": lambda: (xn_lo_ready, n * KT + i + 1),
                "dt": lambda: (dt_exp, n + 1),
                "conv": lambda: (conv_done, n * NV + CONV_ORDER.index(i) + 1),
                "dtok": lambda: (dtok_step, 3 * n + 2),
                "cs": lambda: (cs_s_ready, 4 * n + 4),
                "csT": lambda: (csT_ready, n + 1),
                "z": lambda: (sz_ready, n * NM + i + 1),
                "gu": lambda: (fuse_ready, n + 1),
                "down": lambda: (ffn_out, 2 * n + 2),
                "xtok": lambda: (xdt_ready, n + 1),
                "btcb": lambda: (cbm_ready, 4 * n + 4),
                "s": lambda: (state_ready, states_before(n) + 1),
                "inter": lambda: (inter_ready, n + 1),
                "y": lambda: (y_ready, n + 1),
                "out": lambda: (res_ready, n + 1),
            }[kind or name]()

        block = ctx.enter_context(nc.Block())

        @block.sync
        def _(sp):
            w_rows = w_in[0:10 * P, :].rearrange("(r p) k -> p r k", p=P)

            def load_x(h):
                b, half = divmod(h, 2)
                sp.dma_start(x_sb[:, 2 * h:2 * h + 2, :],
                             x[b, half * SH:(half + 1) * SH, :].rearrange("(t p) k -> p t k", p=P)).then_inc(x_in[h], 16)

            load_x(0)
            load_x(1)
            sp.dma_start(w_nat[:, 8:10, :], w_rows[:, 8:10, :]).then_inc(w_b_in, 16)
            sp.dma_start(w_dt_nat[0:H, :], w_in[10 * P:10 * P + H, :]).then_inc(w_b_in, 16)
            sp.dma_start(w_nat[:, 4:8, :], w_rows[:, 4:8, :]).then_inc(w_a_in, 16)
            sp.dma_start(gate_nat.rearrange("p (k i) -> p k i", i=I),
                         gate_w.rearrange("(k p) i -> p k i", p=P)).then_inc(gate_in, 16)
            sp.dma_start(wo_nat, w_out.rearrange("(r p) c -> p r c", p=P)).then_inc(w_out_in, 16)
            sp.dma_start(up_nat.rearrange("p (k i) -> p k i", i=I),
                         up_w.rearrange("(k p) i -> p k i", p=P)).then_inc(up_in, 16)
            sp.dma_start(w_nat[:, 0:4, :], w_rows[:, 0:4, :]).then_inc(w_c_in, 16)
            load_x(2)
            load_x(3)
            sp.dma_start(down_nat.rearrange("p (k i) -> p k i", i=DIM),
                         down_w.rearrange("(k p) i -> p k i", p=P)).then_inc(down_in, 16)
            with nc.allow_non_contiguous_dma(reason="small parameters"):
                for m in range(NM):
                    sp.dma_start(dcol[:, m:m + 1], bass.AP(tensor=d_skip.tensor, offset=m * (P // HP),
                                                           ap=[[1, P // HP], [0, HP], [1, 1]])).then_inc(d_skip_in, 16)
                sp.dma_start(gscale[:, :], gate_scale.rearrange("(m p) -> p m", p=P)).then_inc(scales_in, 16)
                sp.dma_start(uscale[:, :], up_scale.rearrange("(m p) -> p m", p=P)).then_inc(scales_in, 16)
                sp.dma_start(dscale[:, :], down_scale.partition_broadcast(P)).then_inc(scales_in, 16)

            def store_cs(b):
                sp.wait_ge(csT_ready, b + 1)
                sp.dma_start(cs_dram[b], csT[:, :]).then_inc(cs_stored, 16)

            def spread_cs(n):
                b, t = divmod(n, NT)
                sp.wait_ge(cs_stored, 16 * (b + 1))
                if n >= 3:
                    wait_filled(sp, "y", n - 3)
                elif n == 0:
                    for name in ("w_a1", "w_b1", "w_c1"):
                        wait_filled(sp, name)
                elif n == 1:
                    wait_filled(sp, "wo_1")
                    sp.wait_ge(ffn_q_ready, 3)
                for j in range(2):
                    src = bass.AP(tensor=cs_dram.tensor, offset=(b * H + j) * S + t * P,
                                  ap=[[0, LC], [2 * S, NG], [1, P]])
                    sp.dma_start(mix[j * LC:(j + 1) * LC, n % 3, :, :], src).then_inc(cs_spread[n % 3], 16)

            def store(n):
                b, t = divmod(n, NT)
                sp.wait_ge(res_ready, n + 1)
                sp.dma_start(out[b, t * P:(t + 1) * P, :], x_sb[:, n, :]).then_inc(stored, 16)

            store_cs(0)
            for n in range(3):
                spread_cs(n)
            store_cs(1)
            for n in range(3, NN):
                spread_cs(n)
                if n >= 5:
                    store(n - 5)
            for n in range(NN - 5, NN):
                store(n)
            sp.wait_ge(stored, 16 * NN)

        @block.gpsimd
        def _(pool):
            pool.memset(ident[:, :], 0.0).then_inc(ident_zero, 1)
            pool.memset(minus_half[:, :], -0.5).then_inc(half_ready, 1)
            pool.memset(tri[:, :], 1.0).then_inc(masks_step, 1)
            pool.memset(suffix[:, :], 1.0).then_inc(masks_step, 1)
            pool.memset(whole[:, :, :], 0.0).then_inc(masks_step, 1)
            pool.wait_ge(ident_zero, 1)
            pool.affine_select(out=ident[:, :], in_=ident[:, :], compare_op=ALU.not_equal, fill=1.0,
                               base=0, pattern=[[-1, P]], channel_multiplier=1).then_inc(ident_ready, 1)
            pool.wait_ge(masks_step, 3)
            pool.affine_select(out=tri[:, :], in_=tri[:, :], compare_op=ALU.is_ge, fill=0.0, base=0,
                               pattern=[[1, P]], channel_multiplier=-1).then_inc(masks_step, 1)
            pool.affine_select(out=suffix[:, :], in_=suffix[:, :], compare_op=ALU.is_ge, fill=0.0, base=-1,
                               pattern=[[-1, P]], channel_multiplier=1).then_inc(masks_step, 1)

            def reciprocal_std(b):
                pool.wait_ge(var_ready, b + 1)
                pool.wait_ge(half_ready, 1)
                pool.tensor_tensor(rstd[:, :], var_eps[:, :], minus_half[:, :], ALU.pow).then_inc(rstd_ready, 1)

            def round_weights(i, nat, q, arrived):
                pool.wait_ge(magic_ready, i + 1)
                pool.wait_ge(arrived, 16)
                pool.tensor_tensor(nat, nat, magic[i % 2], ALU.add).then_inc(added, 1)
                pool.wait_ge(added, i + 1)
                pool.tensor_tensor(q[:, :, :].rearrange("p k i -> p (k i)"), nat, magic[i % 2],
                                   ALU.subtract).then_inc(ffn_q_ready, 1)

            def segments(n, parts=(0, 1)):
                b, t = divmod(n, NT)
                pool.wait_ge(cs_spread[n % 3], 32 * (n // 3 + 1))
                pool.wait_ge(cs_s_ready, 4 * (b + 1))
                for part in parts:
                    gs = slice(part * NG // 2, (part + 1) * NG // 2)
                    seg = mix[:, n % 3, gs, :].rearrange("p g (e l) -> p g e l", l=LC)
                    at_s = cs_s[:, b, gs, 2 * t:2 * t + 2]
                    pool.tensor_tensor(seg, at_s.unsqueeze(3).broadcast_to([P, NG // 2, 2, LC]), seg,
                                       ALU.subtract).then_inc(seg_ready, 1)

            def decayed_x(n):
                b, t = divmod(n, NT)
                pool.wait_ge(decays_ready, 3 * (b + 1))
                pool.wait_ge(xdt_ready, n + 1)
                if n >= 2:
                    wait_states_made(pool, n - 2)
                pool.tensor_tensor(xw[:, n % 2, :].rearrange("p (h q) -> p h q", q=HP),
                                   xdt[:, n % 2, :].rearrange("p (h q) -> p h q", q=HP),
                                   by_head(decay_out[:, b, t, :], [P, H, HP]), ALU.mult).then_inc(xw_ready, 1)

            def fuse_low(k):
                pool.wait_ge(hi_ready, k + 1)
                if k >= 3:
                    pool.wait_ge(down_done, k - 2)
                pool.tensor_tensor(fuse_lo[:, k % 3, :], fuse[:, k % 3, :], fuse_hi[:, k % 3, :].bitcast(F32),
                                   ALU.subtract).then_inc(lo_ready, 1)

            def add_ffn(n):
                pool.wait_ge(ffn_out, n + 1)
                pool.tensor_tensor(x_sb[:, n, :], x_sb[:, n, :], ffn[:, n % 2, :], ALU.add).then_inc(ffn_added, 1)

            def sum_squares(n):
                pool.wait_ge(square_ready, n + 1)
                pool.tensor_tensor(sq2[:, :, :], square[:, 0:2, :], square[:, 2:4, :], ALU.add).then_inc(sq2_ready, 1)
                pool.wait_ge(sq2_ready, n + 1)
                if n:
                    wait_filled(pool, "out", n - 1)
                pool.tensor_tensor(sqsum[:, :], sq2[:, 0, :], sq2[:, 1, :], ALU.add).then_inc(sqsum_ready, 1)

            def reciprocal_rms(n):
                pool.wait_ge(ms_ready, n + 1)
                pool.tensor_tensor(rrms[:, n % 2:n % 2 + 1], ms[:, n % 2:n % 2 + 1], minus_half[:, 0:1],
                                   ALU.pow).then_inc(rrms_ready, 1)

            def zero_inter(b):
                if b:
                    wait_filled(pool, "y", b * NT - 2)
                pool.memset(inter[0:LC, b * NT % 2, :], 0.0).then_inc(inter_zero, 1)

            reciprocal_std(0)
            round_weights(0, gate_nat, gate_q, gate_in)
            reciprocal_std(1)
            round_weights(1, up_nat, up_q, up_in)
            round_weights(2, down_nat, down_q, down_in)
            pool.memset(xdiag[:, :, :, :], 0.0).then_inc(zeros_ready, 1)
            pool.memset(btok[:, :, :, :], 0.0).then_inc(zeros_ready, 1)
            zero_inter(0)
            for j in range(NP // 2):
                fuse_low(j)
                if j == NI + 1:
                    add_ffn(0)
                    add_ffn(1)
                if j in (NI - 1, NI):
                    segments(0, (j - NI + 1,))
                if j == NI + 2:
                    decayed_x(0)
                if j in (NI + 3, NI + 4):
                    segments(1, (j - NI - 3,))
            fuse_low(NP // 2)
            fuse_low(NP // 2 + 1)
            for n in range(NN + 1):
                k = NP // 2 + 2 * n
                if 0 < n < NN:
                    sum_squares(n - 1)
                if n == 0:
                    decayed_x(1)
                if k + 2 < NP:
                    fuse_low(k + 2)
                if 0 < n < NN - 1:
                    decayed_x(n + 1)
                if n:
                    reciprocal_rms(n - 1)
                if k + 3 < NP:
                    fuse_low(k + 3)
                if n + 2 < NN:
                    segments(n + 2)
                if n == NT - 1:
                    zero_inter(1)
                if n == 1:
                    add_ffn(2)
                    add_ffn(3)
                if n == 3:
                    add_ffn(4)
                    add_ffn(5)
                if n == 6:
                    add_ffn(6)
                    add_ffn(7)

        @block.tensor
        def _(pe):
            def claim(name, n=0):
                k, before, _ = JOB[name, n]
                if before:
                    pe.wait_ge(*read_out(*before))
                return bank[k]

            def fill(name, n=0):
                return full[JOB[name, n][0]]

            def turn(dst, src, n):
                return pe.transpose(dst, src, ident[0:n, 0:n])

            def turn_w_in(name, arrived, count, blocks):
                pe.wait_ge(arrived, count)
                for k in range(KT):
                    to = claim(f"{name}{k}")
                    for n, r in enumerate(blocks):
                        rows = P if r < 10 else H
                        src = w_nat[:, r, k * P:(k + 1) * P] if r < 10 else w_dt_nat[0:H, k * P:(k + 1) * P]
                        last = turn(to[:, n * P:n * P + rows], src, rows)
                    last.then_inc(fill(f"{name}{k}"), 1)

            def turn_w_out():
                pe.wait_ge(w_out_in, 16)
                for n in range(2):
                    to = claim(f"wo_{n}")
                    for i in range(2):
                        for r in range(2):
                            m = 2 * n + i
                            last = turn(to[:, i * DIM + r * P:i * DIM + (r + 1) * P],
                                        wo_nat[:, r, m * P:(m + 1) * P], P)
                    last.then_inc(fill(f"wo_{n}"), 1)

            def turn_xn(b):
                for k in range(KT):
                    to = claim(f"xn_{k}", b)
                    for t in range(NT):
                        pe.wait_ge(xn_ready, b * NT + t + 1)
                        last = turn(to[:, t * P:(t + 1) * P], xn[:, t, k * P:(k + 1) * P], P)
                    last.then_inc(fill(f"xn_{k}", b), 1)

            def in_projection(name, b, col):
                to = claim(name, b)
                ops = [(w, a, k) for w, a in ((w_hi, xn_hi), (w_lo, xn_hi), (w_hi, xn_lo)) for k in range(KT)]
                for n, (w, a, k) in enumerate(ops):
                    last = pe.matmul(to[:, :], w[:, k, col:col + P], a[:, b, k, :],
                                     start=(n == 0), stop=(n == len(ops) - 1))
                last.then_inc(fill(name, b), 1)

            parts = (da_hi, da_mid, da_lo)

            def sums_of_da(b):
                to = claim("csT", b)
                pe.wait_ge(masks_ready, 7)
                pe.wait_ge(da_split, b + 1)
                for t in range(NT):
                    for n, part in enumerate(parts):
                        last = pe.matmul(to[0:H, t * P:(t + 1) * P], part[:, t, :], tri[:, :],
                                         start=(n == 0), stop=(n == 2))
                last.then_inc(fill("csT", b), 1)
                to = claim("cs", b)
                for t in range(NT):
                    for n, part in enumerate(parts):
                        pe.matmul(to[:, t * H:(t + 1) * H], tri[:, :], part[:, t, :], start=(n == 0), stop=(n == 2))
                for t in range(NT):
                    for n, part in enumerate(parts):
                        pe.matmul(to[:, P + t * H:P + (t + 1) * H], suffix[:, :], part[:, t, :],
                                  start=(n == 0), stop=(n == 2))
                for c in range(NC):
                    for n, part in enumerate(parts):
                        last = pe.matmul(to[:, 2 * P + c * H:2 * P + (c + 1) * H], whole[:, c % 2, :],
                                         part[:, c // 2, :], start=(n == 0), stop=(n == 2))
                last.then_inc(fill("cs", b), 1)

            def turn_dt(b):
                to = claim("dtok", b)
                pe.wait_ge(da_ready, b + 1)
                for t in range(NT):
                    last = pe.transpose(to[:, t * 2 * H:(t + 1) * 2 * H], dtA[2 * H:4 * H, t * P:(t + 1) * P],
                                        ident[2 * H:4 * H, 2 * H:4 * H])
                last.then_inc(fill("dtok", b), 1)

            def gate_up(k):
                h, i = divmod(k, NI)
                b, half = divmod(h, 2)
                if k == 0:
                    pe.wait_ge(ffn_q_ready, 2)
                to = claim("gu", k)
                for at, q in ((0, gate_q), (SH, up_q)):
                    for n, (part, kt) in enumerate([(part, kt) for kt in range(KT) for part in (xn_hi, xn_lo)]):
                        last = pe.matmul(to[:, at:at + SH], q[:, kt, i * P:(i + 1) * P],
                                         part[:, b, kt, half * SH:(half + 1) * SH],
                                         start=(n == 0), stop=(n == 2 * KT - 1))
                last.then_inc(fill("gu", k), 1)

            def down(k):
                h, i = divmod(k, NI)
                to = claim("down", h) if i == 0 else bank_of("down", h)
                if k == 0:
                    pe.wait_ge(ffn_q_ready, 3)
                pe.wait_ge(lo_ready, k + 1)
                for t in range(2):
                    for part in (fuse_hi, fuse_lo):
                        last = pe.matmul(to[:, t * DIM:(t + 1) * DIM], part[:, k % 3, t * P:(t + 1) * P],
                                         down_q[:, i, :], start=(i == 0 and t == 0 and part is fuse_hi),
                                         stop=(i == NI - 1 and part is fuse_lo), skip_group_check=True)
                last.then_inc(down_done, 1)

            def turn_tokens(n):
                b, t = divmod(n, NT)
                cols = slice(t * P, (t + 1) * P)
                to = claim("xtok", n)
                for m in range(NM):
                    last = turn(to[:, m * P:(m + 1) * P], xbc[:, b, m, cols], P)
                last.then_inc(fill("xtok", n), 1)
                to = claim("btcb", n)
                turn(to[:, 0:P], xbc[:, b, 4, cols], P)
                pe.matmul(to[:, P:2 * P], xbc[:, b, 4, cols], xbc[:, b, 5, cols],
                          start=True, stop=True).then_inc(fill("btcb", n), 1)

            def chunk_state(c):
                n, e = divmod(c, 2)
                to = claim("s", c)
                if e == 0:
                    pe.wait_ge(btok_ready, 2 * n + 2)
                    pe.wait_ge(xw_ready, n + 1)
                pe.matmul(to[:, :], btok[:, n % 2, e, :], xw[:, n % 2, :], start=True,
                          stop=True).then_inc(fill("s", c), 1)

            def from_states(n):
                b, t = divmod(n, NT)
                to = claim("inter", n)
                for e in range(2):
                    if t or e:
                        c = 2 * n + e
                        pe.wait_ge(state_ready, states_before(c))
                        at = t * P + e * LC
                        pe.matmul(to[e * LC:(e + 1) * LC, :], xbc[:, b, 5, at:at + LC], state[:, c % 3, :],
                                  start=True, stop=True).then_inc(inter_done, 1)

            def within_chunks(n):
                b, t = divmod(n, NT)
                to = claim("y", n)
                if n == 0:
                    pe.wait_ge(diag_ready, NM)
                for m in range(NM):
                    pe.matmul(to[:, m * P:(m + 1) * P], diag_d[:, m, :], xbc[:, b, m, t * P:(t + 1) * P],
                              start=(m == 0), stop=False, skip_group_check=True)
                pe.wait_ge(xdiag_ready, 4 * n + 4)
                for m in range(NM):
                    if m % 2 == 0:
                        pe.wait_ge(mix_ready, 2 * n + m // 2 + 1)
                    for e in range(2):
                        for i in range(GM):
                            g = m * GM + i
                            at = m * P + e * LC
                            pe.matmul(to[32 * i:32 * (i + 1), at:at + LC],
                                      xdiag[:, n % 2, e, 32 * g:32 * (g + 1)],
                                      mix[:, n % 3, g, e * LC:(e + 1) * LC],
                                      start=False, stop=False, skip_group_check=True)
                pe.wait_ge(inter_ready, n + 1)
                for m in range(NM):
                    last = pe.matmul(to[:, m * P:(m + 1) * P], inter[:, n % 2, m * P:(m + 1) * P], ident[:, :],
                                     start=False, stop=True, skip_group_check=True)
                last.then_inc(fill("y", n), 1)

            def out_projection(n):
                b, t = divmod(n, NT)
                to = claim("out", n)
                if n == 0:
                    pe.wait_ge(wo_ready, NM)
                pe.wait_ge(y_ready, n + 1)
                for m in range(NM):
                    if n == NN - 1 and m == NM // 2:
                        sum_of_last_squares()
                    last = pe.matmul(to[:, 0:DIM], sz[:, b, m, t * P:(t + 1) * P], woT[:, m, :], start=(m == 0),
                                     stop=(m == NM - 1), skip_group_check=True)
                if n == NN - 1:
                    last.then_inc(fill("out", n), 1)

            def sum_of_last_squares():
                to = claim("squares", NN - 1)
                pe.wait_ge(square_ready, NN)
                for m in range(NM):
                    last = pe.matmul(to[:, DIM:DIM + 1], square[:, m, :], ones[:, :], start=(m == 0),
                                     stop=(m == NM - 1))
                last.then_inc(fill("squares", NN - 1), 1)

            def sum_of_squares(n):
                pe.wait_ge(sqsum_ready, n + 1)
                pe.matmul(bank_of("out", n)[:, DIM:DIM + 1], sqsum[:, :], ones[:, :], start=False, stop=True,
                          skip_group_check=True).then_inc(fill("out", n), 1)

            def convolved(n, b):
                i = CONV_ORDER[n]
                in_projection(f"conv_{i}", b, HID + i * P)

            def dt_projection(b):
                in_projection("dt", b, 2 * HID + 2 * NS + H - P)

            pe.wait_ge(ident_ready, 1)
            turn_w_in("w_b", w_b_in, 32, (8, 9, 10))
            turn_xn(0)
            turn_w_in("w_a", w_a_in, 16, range(4, 8))
            pe.wait_ge(w_lo_ready, 2)
            pe.wait_ge(xn_lo_ready, KT)
            dt_projection(0)
            convolved(0, 0)
            convolved(1, 0)
            turn_w_out()
            pe.wait_ge(w_lo_ready, 4)
            convolved(2, 0)
            turn_dt(0)
            turn_w_in("w_c", w_c_in, 16, range(0, 4))
            convolved(3, 0)
            convolved(4, 0)
            convolved(5, 0)
            turn_xn(1)
            sums_of_da(0)
            pe.wait_ge(xn_lo_ready, 2 * KT)
            dt_projection(1)
            pe.wait_ge(w_lo_ready, 6)
            for i in range(NM):
                in_projection(f"z_{i}", 0, i * P)
            gate_up(0)
            convolved(0, 1)
            gate_up(1)
            gate_up(2)
            convolved(1, 1)
            for j in range(NP // 2):
                if j:
                    gate_up(j + 2)
                if j + 2 < NV:
                    convolved(j + 2, 1)
                elif j in Z_STEPS:
                    in_projection(f"z_{Z_STEPS.index(j)}", 1, Z_STEPS.index(j) * P)
                if j:
                    down(j - 1)
                if j == 2:
                    turn_dt(1)
                if j == NV:
                    pe.wait_ge(silu_done, NV)
                    turn_tokens(0)
                if j == NV + 4:
                    sums_of_da(1)
                if j == NV + 5:
                    turn_tokens(1)
            down(NP // 2 - 1)
            for n in range(NN):
                k = NP // 2 + 2 * n
                chunk_state(2 * n)
                if n and n + 1 < NN:
                    if n + 1 == NT:
                        pe.wait_ge(silu_done, 2 * NV)
                    turn_tokens(n + 1)
                if k + 2 < NP:
                    gate_up(k + 2)
                if n:
                    out_projection(n - 1)
                if k < NP:
                    down(k)
                if n % NT < NT - 1:
                    chunk_state(2 * n + 1)
                if k + 3 < NP:
                    gate_up(k + 3)
                if n:
                    sum_of_squares(n - 1)
                if k < NP:
                    down(k + 1)
                from_states(n)
                within_chunks(n)
            out_projection(NN - 1)

        @block.scalar
        def _(act):
            with nc.allow_non_contiguous_dma(reason="small parameters"):
                act.dma_start(heads[3 * H:4 * H, 0:1],
                              dt_bias.rearrange("(h o) -> h o", o=1)).then_inc(front_params_in, 16)
                act.dma_start(heads[3 * H:4 * H, 1:2],
                              a_log.rearrange("(h o) -> h o", o=1)).then_inc(front_params_in, 16)
                act.dma_start(convw[:, :, :], conv_w.rearrange("(m p) k -> p m k", p=P)).then_inc(front_params_in, 16)
                act.dma_start(convb[:, :], conv_b.rearrange("(m p) -> p m", p=P)).then_inc(front_params_in, 16)
                act.dma_start(normw[:, :], norm_w.rearrange("(m p) -> p m", p=P)).then_inc(norm_w_in, 16)

            def weights_high(name, col, width):
                for k in range(KT):
                    src = wait_filled(act, f"{name}{k}")
                    act.activation(w_hi[:, k, col:col + width], src[:, 0:width], ACT.Copy).then_inc(w_hi_ready, 1)

            def xn_high(b):
                for k in range(KT):
                    src = wait_filled(act, f"xn_{k}", b)
                    act.activation(xn_hi[:, b, k, :], src[:, :], ACT.Copy).then_inc(xn_hi_ready, 1)

            def layer_norm():
                act.wait_ge(shift_ready, 1)
                wait_filled(act, "xn_1", 0)
                for t in range(NT):
                    act.activation(xn[:, t, :], x_sb[:, NT + t, :], ACT.Identity, bias=shift[:, t:t + 1],
                                   scale=rstd[:, t:t + 1]).then_inc(xn_ready, 1)

            def softplus(b, between=lambda: None):
                src = wait_filled(act, "dt", b)
                if b:
                    wait_filled(act, "dtok", b - 1)
                act.activation(dtA[3 * H:4 * H, :], src[3 * H:4 * H, :], ACT.Exp,
                               bias=heads[3 * H:4 * H, 0:1]).then_inc(dt_exp, 1)
                between()
                act.wait_ge(dt_exp, b + 1)
                act.activation(dtA[3 * H:4 * H, :], dtA[3 * H:4 * H, :], ACT.Ln, bias=1.0).then_inc(dt_ln, 1)

            def last_tap(n, b):
                i = CONV_ORDER[n]
                src = wait_filled(act, f"conv_{i}", b)
                if b and n == 0:
                    act.wait_ge(ffn_q_ready, 2)
                act.activation(xbc[:, b, i, :], src[:, :], ACT.Identity, bias=convb[:, i:i + 1],
                               scale=convw[:, i, TAPS - 1:TAPS]).then_inc(tap_done, 1)

            def w_out_normed():
                act.wait_ge(norm_w_in, 16)
                for m in range(NM):
                    src = wait_filled(act, f"wo_{m // 2}")
                    act.activation(woT[:, m, :], src[:, (m % 2) * DIM:(m % 2 + 1) * DIM], ACT.Copy,
                                   scale=normw[:, m:m + 1]).then_inc(wo_ready, 1)

            def diagonals():
                act.wait_ge(d_skip_in, 16 * NM)
                for m in range(NM):
                    act.activation(diag_d[:, m, :], ident[:, :], ACT.Copy, scale=dcol[:, m:m + 1]).then_inc(diag_ready, 1)

            def cs_by_head(b):
                src = wait_filled(act, "csT", b)
                if b:
                    act.wait_ge(cs_stored, 16 * b)
                act.activation(csT[:, :], src[0:H, :], ACT.Copy).then_inc(csT_ready, 1)

            def decays(b):
                src = wait_filled(act, "cs", b)
                act.activation(decay_in[:, b, :, :], src[:, 0:P].rearrange("p (t h) -> p t h", h=H),
                               ACT.Exp).then_inc(decays_ready, 1)
                act.activation(decay_out[:, b, :, :], src[:, P:2 * P].rearrange("p (t h) -> p t h", h=H),
                               ACT.Exp).then_inc(decays_ready, 1)
                act.activation(decay_all[:, b, :, :], src[:, 2 * P:4 * P].rearrange("p (c h) -> p c h", h=H),
                               ACT.Exp).then_inc(decays_ready, 1)

            def silu_conv(n, b):
                i = CONV_ORDER[n]
                act.wait_ge(conv_done, b * NV + n + 1)
                act.activation(xbc[:, b, i, :], xbc[:, b, i, :], ACT.Silu).then_inc(silu_done, 1)

            def silu_z(i, b):
                src = wait_filled(act, f"z_{i}", b)
                if b and i == 0:
                    act.wait_ge(ffn_q_ready, 3)
                act.activation(sz[:, b, i, :], src[:, :], ACT.Silu).then_inc(sz_ready, 1)

            def gate(k):
                i = k % NI
                src = wait_filled(act, "gu", k)
                if k >= 3:
                    act.wait_ge(lo_ready, k - 2)
                if k < BY_TANH:
                    act.activation(fuse[:, k % 3, :], src[:, 0:SH], ACT.Silu,
                                   scale=gscale[:, i:i + 1]).then_inc(gate_ready, 1)
                else:
                    if k == BY_TANH:
                        act.wait_ge(half_scales_ready, 1)
                    act.activation(fuse[:, k % 3, :], src[:, 0:SH], ACT.Tanh,
                                   scale=half_gscale[:, i:i + 1]).then_inc(gate_ready, 1)

            def fuse_high(k):
                act.wait_ge(fuse_ready, k + 1)
                if k >= 3:
                    act.wait_ge(down_done, k - 2)
                act.activation(fuse_hi[:, k % 3, :], fuse[:, k % 3, :], ACT.Copy).then_inc(hi_ready, 1)

            def b_tokens(n):
                src = wait_filled(act, "btcb", n)
                act.wait_ge(zeros_ready, 2)
                if n >= 2:
                    wait_states_made(act, n - 2)
                for e in range(2):
                    rows = slice(e * LC, (e + 1) * LC)
                    act.activation(btok[rows, n % 2, e, :], src[rows, 0:P], ACT.Copy).then_inc(btok_ready, 1)

            def spread_x(n):
                act.wait_ge(xdt_ready, n + 1)
                act.wait_ge(zeros_ready, 2)
                if n >= 2:
                    wait_filled(act, "y", n - 2)
                pick = lambda ap: ap.rearrange("p (g j q) -> p g j q", j=2, q=HP)
                for e in range(2):
                    for j in range(2):
                        act.activation(pick(xdiag[j * LC:(j + 1) * LC, n % 2, e, :])[:, :, j, :],
                                       pick(xdt[e * LC:(e + 1) * LC, n % 2, :])[:, :, j, :],
                                       ACT.Copy).then_inc(xdiag_ready, 1)

            def cap_segments(n, part):
                seg = mix[:, n % 3, part * NG // 2:(part + 1) * NG // 2, :]
                act.wait_ge(seg_ready, 2 * n + part + 1)
                act.activation(seg, seg, ACT.Relu).then_inc(seg_capped, 1)

            def exp_segments(n, part):
                seg = mix[:, n % 3, part * NG // 2:(part + 1) * NG // 2, :]
                act.wait_ge(seg_capped, 2 * n + part + 1)
                act.activation(seg, seg, ACT.Exp, scale=-1.0).then_inc(seg_exp, 1)

            def squares(n):
                b, t = divmod(n, NT)
                act.wait_ge(y_ready, n + 1)
                if n:
                    act.wait_ge(sq2_ready, n)
                act.activation(square[:, :, :], sz[:, b, :, t * P:(t + 1) * P], ACT.Square).then_inc(square_ready, 1)

            weights_high("w_b", HID + 512, 2 * P + H)
            xn_high(0)
            act.wait_ge(front_params_in, 4 * 16)
            act.activation(heads[3 * H:4 * H, 2:3], heads[3 * H:4 * H, 1:2], ACT.Exp).then_inc(a_exp, 1)
            weights_high("w_a", HID, 512)
            softplus(0)
            last_tap(0, 0)
            last_tap(1, 0)
            w_out_normed()
            last_tap(2, 0)
            weights_high("w_c", 0, 512)
            last_tap(3, 0)
            last_tap(4, 0)
            layer_norm()
            last_tap(5, 0)
            xn_high(1)
            cs_by_head(0)
            decays(0)
            softplus(1)
            silu_conv(0, 0)
            silu_conv(1, 0)
            for i in range(NM):
                silu_z(i, 0)
            act.wait_ge(scales_in, 3 * 16)
            gate(0)
            gate(1)
            last_tap(0, 1)
            silu_conv(2, 0)
            silu_conv(3, 0)
            fuse_high(0)
            fuse_high(1)
            gate(2)
            last_tap(1, 1)
            fuse_high(2)
            for j in range(NP // 2):
                if j:
                    gate(j + 2)
                if j + 2 < NV:
                    last_tap(j + 2, 1)
                elif j in Z_STEPS:
                    silu_z(Z_STEPS.index(j), 1)
                if j == NP // 2 - 2:
                    cap_segments(0, 0)
                if j == NP // 2 - 1:
                    exp_segments(0, 0)
                if j:
                    fuse_high(j + 2)
                if 0 < j <= NV - NM:
                    silu_conv(NM + j - 1, 0)
                if NM <= j < NM + NV:
                    silu_conv(j - NM, 1)
                if j == NM:
                    diagonals()
                if j == NV:
                    b_tokens(0)
            for n in range(NN):
                k = NP // 2 + 2 * n
                if n:
                    squares(n - 1)
                if k + 2 < NP:
                    gate(k + 2)
                if n == 0:
                    cs_by_head(1)
                    decays(1)
                    cap_segments(0, 1)
                    exp_segments(0, 1)
                if n + 1 < NN:
                    b_tokens(n + 1)
                if k + 2 < NP:
                    fuse_high(k + 2)
                if n == 0:
                    gate(k + 3)
                    cap_segments(n + 1, 0)
                    exp_segments(n + 1, 0)
                if n + 1 < NN:
                    spread_x(n + 1)
                if n and k + 3 < NP:
                    gate(k + 3)
                if k + 3 < NP:
                    fuse_high(k + 3)
                if n + 1 < NN:
                    for part in range(n == 0, 2):
                        cap_segments(n + 1, part)
                        exp_segments(n + 1, part)
            squares(NN - 1)

        @block.vector
        def _(dve):
            def masks():
                dve.wait_ge(masks_step, 5)
                dve.memset(whole[0:LC, 0, :], 1.0).then_inc(masks_ready, 1)
                dve.memset(whole[LC:P, 1, :], 1.0).then_inc(masks_ready, 1)
                dve.memset(tri[0:LC, LC:P], 0.0).then_inc(masks_ready, 1)
                dve.memset(suffix[LC:P, 0:LC], 0.0).then_inc(masks_ready, 1)
                for e in range(2):
                    dve.tensor_copy(causal[e * LC:(e + 1) * LC, :],
                                    tri[e * LC:(e + 1) * LC, e * LC:(e + 1) * LC]).then_inc(masks_ready, 1)
                dve.memset(ones[:, :], 1.0).then_inc(masks_ready, 1)

            def layer_norm_stats(b):
                for t in range(NT):
                    if t % 2 == 0:
                        dve.wait_ge(x_in[2 * b + t // 2], 16)
                    if b and t == 0:
                        dve.wait_ge(xn_ready, NT * b)
                    dve.bn_stats(stats[:, t, :], x_sb[:, b * NT + t, :]).then_inc(stats_done, 1)
                for t in range(NT):
                    dve.wait_ge(stats_done, b * NT + t + 1)
                    dve.bn_aggr(meanvar[:, t, :], stats[:, t, :]).then_inc(meanvar_done, 1)
                dve.wait_ge(meanvar_done, NT * (b + 1))
                dve.tensor_scalar(var_eps[:, :], meanvar[:, :, 1], LN_EPS, None, ALU.add).then_inc(var_ready, 1)

            def layer_norm(b):
                dve.wait_ge(rstd_ready, b + 1)
                if b:
                    wait_filled(dve, "xn_1", b - 1)
                for t in range(NT):
                    dve.tensor_scalar(xn[:, t, :], x_sb[:, b * NT + t, :], meanvar[:, t, 0:1], rstd[:, t:t + 1],
                                      ALU.subtract, ALU.mult).then_inc(xn_ready, 1)

            def minus_mean(b):
                dve.wait_ge(rstd_ready, b + 1)
                dve.scalar_tensor_tensor(out=shift[:, :], in0=meanvar[:, :, 0], scalar=-1.0, in1=rstd[:, :],
                                         op0=ALU.mult, op1=ALU.mult).then_inc(shift_ready, 1)

            def weights_low(name, n, col, width):
                for k in range(KT):
                    src = wait_filled(dve, f"{name}{k}")
                    dve.wait_ge(w_hi_ready, n + k + 1)
                    dve.tensor_tensor(w_lo[:, k, col:col + width], src[:, 0:width],
                                      w_hi[:, k, col:col + width].bitcast(F32),
                                      ALU.subtract).then_inc(w_lo_ready, 1)

            def magic_numbers(i, nat, arrived):
                dve.wait_ge(arrived, 16)
                if i >= 2:
                    dve.wait_ge(ffn_q_ready, i - 1)
                dve.tensor_scalar(magic[i % 2].bitcast(U32), nat.bitcast(U32), EXPONENT, None,
                                  ALU.bitwise_and).then_inc(expo_step, 1)
                dve.wait_ge(expo_step, i + 1)
                dve.tensor_scalar(magic[i % 2], magic[i % 2], E4M3_MIN_NORMAL, ROUND_TO_E4M3, ALU.max,
                                  ALU.mult).then_inc(magic_ready, 1)

            def xn_low(b):
                for k in range(KT):
                    src = wait_filled(dve, f"xn_{k}", b)
                    dve.wait_ge(xn_hi_ready, b * KT + k + 1)
                    dve.tensor_tensor(xn_lo[:, b, k, :], src[:, :], xn_hi[:, b, k, :].bitcast(F32),
                                      ALU.subtract).then_inc(xn_lo_ready, 1)

            def time_steps(b):
                dve.wait_ge(dt_ln, b + 1)
                dt = dtA[3 * H:4 * H, :]
                dve.tensor_scalar(dt, dt, DT_MIN, DT_MAX, ALU.max, ALU.min).then_inc(dt_clipped, 1)
                dve.wait_ge(dt_clipped, b + 1)
                dve.tensor_scalar(dtA[2 * H:3 * H, :], dt, heads[3 * H:4 * H, 3:4], None,
                                  ALU.mult).then_inc(da_ready, 1)

            def other_taps(*ns, b):
                for k in range(1, TAPS):
                    for at, n in enumerate(ns):
                        i = CONV_ORDER[n]
                        src = bank_of(f"conv_{i}", b)
                        if k == 1:
                            dve.wait_ge(tap_done, b * NV + n + 1)
                        else:
                            dve.wait_ge(tap_step, (b * NV + ns[0]) * (TAPS - 2) + (k - 2) * len(ns) + at + 1)
                        done = tap_step if k < TAPS - 1 else conv_done
                        dve.scalar_tensor_tensor(out=xbc[:, b, i, k:S], in0=src[:, 0:S - k],
                                                 scalar=convw[:, i, TAPS - 1 - k:TAPS - k], in1=xbc[:, b, i, k:S],
                                                 op0=ALU.mult, op1=ALU.add).then_inc(done, 1)

            def split_da(b):
                src = wait_filled(dve, "dtok", b)[:, 0:NT * 2 * H].rearrange("p (t h) -> p t h", h=2 * H)
                if b:
                    wait_filled(dve, "cs", b - 1)
                da = src[:, :, 0:H]
                dve.tensor_copy(dtok[:, b, :, :], src[:, :, H:2 * H]).then_inc(dtok_ready, 1)
                dve.tensor_copy(da_hi[:, :, :], da).then_inc(dtok_step, 1)
                dve.wait_ge(dtok_step, 3 * b + 1)
                dve.tensor_tensor(rest1[:, :, :], da, da_hi[:, :, :], ALU.subtract).then_inc(dtok_step, 1)
                dve.wait_ge(dtok_step, 3 * b + 2)
                dve.tensor_copy(da_mid[:, :, :], rest1[:, :, :]).then_inc(dtok_step, 1)
                dve.wait_ge(dtok_step, 3 * b + 3)
                dve.tensor_tensor(da_lo[:, :, :], rest1[:, :, :], da_mid[:, :, :], ALU.subtract).then_inc(da_split, 1)

            def chunk_sums(b):
                src = bank_of("cs", b)
                dve.wait_ge(decays_ready, 3 * (b + 1))
                for j in range(2):
                    for e in range(2):
                        rows = slice(e * LC, (e + 1) * LC)
                        pick = lambda ap: ap.rearrange("p t (g j) -> p t g j", j=2)[:, :, :, j]
                        dve.tensor_copy(
                            cs_s[j * LC:(j + 1) * LC, b, :, e:NC:2].rearrange("p g t -> p t g"),
                            pick(src[rows, 0:P].rearrange("p (t h) -> p t h", t=NT))).then_inc(cs_s_ready, 1)

            def x_times_dt(n):
                b, t = divmod(n, NT)
                src = wait_filled(dve, "xtok", n)
                dve.wait_ge(dtok_ready, b + 1)
                if n >= 2:
                    dve.wait_ge(xdiag_ready, 4 * n - 4)
                    dve.wait_ge(xw_ready, n - 1)
                dve.tensor_tensor(xdt[:, n % 2, :].rearrange("p (h q) -> p h q", q=HP),
                                  src[:, :].rearrange("p (h q) -> p h q", q=HP),
                                  by_head(dtok[:, b, t, :], [P, H, HP]), ALU.mult).then_inc(xdt_ready, 1)

            def masked_cb(n):
                dve.wait_ge(masks_ready, 7)
                dve.wait_ge(btok_ready, 2 * n + 2)
                src = bank_of("btcb", n)
                for e in range(2):
                    rows = slice(e * LC, (e + 1) * LC)
                    for j in range(2):
                        dve.tensor_tensor(cbm[j * LC:(j + 1) * LC, n % 2, e, :],
                                          src[rows, P + e * LC:P + (e + 1) * LC], causal[rows, :],
                                          ALU.mult).then_inc(cbm_ready, 1)

            def next_state(c):
                first = c % NC == 0
                b = c // NC
                src = wait_filled(dve, "s", c)
                new = state[:, (c + 1) % 3, :]
                n = states_before(c)
                if n >= 3:
                    dve.wait_ge(inter_done, n - 2)
                if first:
                    dve.tensor_copy(new, src[:, :]).then_inc(state_ready, 1)
                else:
                    dve.wait_ge(state_ready, n)
                    dve.tensor_tensor(new.rearrange("p (h q) -> p h q", q=HP),
                                      state[:, c % 3, :].rearrange("p (h q) -> p h q", q=HP),
                                      by_head(decay_all[:, b, c % NC, :], [P, H, HP]), ALU.mult).then_inc(state_scaled, 1)
                    dve.wait_ge(state_scaled, n - b)
                    dve.tensor_tensor(new, new, src[:, :], ALU.add).then_inc(state_ready, 1)

            def scale_inter(n):
                b, t = divmod(n, NT)
                if n >= 2:
                    wait_filled(dve, "y", n - 2)
                if t == 0:
                    dve.wait_ge(inter_zero, b + 1)
                dve.wait_ge(inter_done, states_before(2 * n + 1))
                rows = slice(LC if t == 0 else 0, P)
                count = P - rows.start
                src = bank_of("inter", n)
                dve.tensor_tensor(inter[rows, n % 2, :].rearrange("p (h q) -> p h q", q=HP),
                                  src[rows, :].rearrange("p (h q) -> p h q", q=HP),
                                  by_head(decay_in[rows, b, t, :], [count, H, HP]), ALU.mult).then_inc(inter_ready, 1)

            def ffn_scales():
                dve.wait_ge(scales_in, 3 * 16)
                dve.tensor_scalar(half_gscale[:, :], gscale[:, :], 0.5, None, ALU.mult).then_inc(half_scales_ready, 1)
                dve.wait_ge(half_scales_ready, 1)
                dve.tensor_tensor(guscale[:, :], half_gscale[:, :], uscale[:, :], ALU.mult).then_inc(scales_ready, 1)

            def fuse_up(k):
                src = bank_of("gu", k)
                scale = uscale
                dve.wait_ge(gate_ready, k + 1)
                if k >= BY_TANH:
                    scale = guscale
                    dve.scalar_tensor_tensor(out=fuse[:, k % 3, :], in0=fuse[:, k % 3, :], scalar=1.0,
                                             in1=src[:, 0:SH], op0=ALU.add, op1=ALU.mult).then_inc(tanh_applied, 1)
                    dve.wait_ge(tanh_applied, k - BY_TANH + 1)
                    dve.wait_ge(scales_ready, 1)
                dve.scalar_tensor_tensor(out=fuse[:, k % 3, :], in0=src[:, SH:2 * SH], scalar=scale[:, k % NI:k % NI + 1],
                                         in1=fuse[:, k % 3, :], op0=ALU.mult, op1=ALU.mult).then_inc(fuse_ready, 1)

            def spread_x(n):
                dve.wait_ge(xdt_ready, n + 1)
                dve.wait_ge(zeros_ready, 2)
                pick = lambda ap: ap.rearrange("p (g j q) -> p g j q", j=2, q=HP)
                for e in range(2):
                    for j in range(2):
                        dve.tensor_copy(pick(xdiag[j * LC:(j + 1) * LC, n % 2, e, :])[:, :, j, :],
                                        pick(xdt[e * LC:(e + 1) * LC, n % 2, :])[:, :, j, :]).then_inc(xdiag_ready, 1)

            def mix_tile(n, part):
                if part == 0:
                    dve.wait_ge(cbm_ready, 4 * n + 4)
                dve.wait_ge(seg_exp, 2 * n + part + 1)
                seg = mix[:, n % 3, part * NG // 2:(part + 1) * NG // 2, :]
                cb = cbm[:, n % 2, :, :].rearrange("p e l -> p (e l)")
                dve.tensor_tensor(seg, seg, cb.unsqueeze(1).broadcast_to([P, NG // 2, P]),
                                  ALU.mult).then_inc(mix_ready, 1)

            def gated(n):
                b, t = divmod(n, NT)
                cols = slice(t * P, (t + 1) * P)
                src = wait_filled(dve, "y", n)
                dve.wait_ge(sz_ready, NM * (b + 1))
                dve.tensor_tensor(sz[:, b, :, cols], src[:, :].rearrange("p (m l) -> p m l", m=NM), sz[:, b, :, cols],
                                  ALU.mult).then_inc(y_ready, 1)

            def ffn_result(h):
                src = wait_filled_down(h)
                for t in range(2):
                    n = 2 * h + t
                    if n >= 2:
                        dve.wait_ge(ffn_added, n - 1)
                    dve.tensor_tensor(ffn[:, n % 2, :], src[:, t * DIM:(t + 1) * DIM], dscale[:, :],
                                      ALU.mult).then_inc(ffn_out, 1)

            def wait_filled_down(h):
                dve.wait_ge(down_done, NI * (h + 1))
                return bank_of("down", h)

            def mean_square(n):
                src = wait_filled(dve, "out" if n < NN - 1 else "squares", n)
                if n >= 2:
                    dve.wait_ge(rrms_ready, n - 1)
                dve.tensor_scalar(ms[:, n % 2:n % 2 + 1], src[:, DIM:DIM + 1], 1.0 / HID, RMS_EPS, ALU.mult,
                                  ALU.add).then_inc(ms_ready, 1)

            def result(n):
                dve.wait_ge(rrms_ready, n + 1)
                dve.wait_ge(ffn_added, n + 1)
                src = wait_filled(dve, "out", n)
                dve.scalar_tensor_tensor(out=x_sb[:, n, :], in0=src[:, 0:DIM], scalar=rrms[:, n % 2:n % 2 + 1],
                                         in1=x_sb[:, n, :], op0=ALU.mult, op1=ALU.add).then_inc(res_ready, 1)

            layer_norm_stats(0)
            layer_norm(0)
            masks()
            weights_low("w_b", 0, HID + 512, 2 * P + H)
            xn_low(0)
            dve.wait_ge(a_exp, 1)
            dve.tensor_scalar(heads[3 * H:4 * H, 3:4], heads[3 * H:4 * H, 2:3], -1.0, None,
                              ALU.mult).then_inc(a_neg, 1)
            magic_numbers(0, gate_nat, gate_in)
            weights_low("w_a", 2, HID, 512)
            dve.wait_ge(a_neg, 1)
            magic_numbers(1, up_nat, up_in)
            time_steps(0)
            layer_norm_stats(1)
            weights_low("w_c", 4, 0, 512)
            minus_mean(1)
            other_taps(0, 1, b=0)
            split_da(0)
            xn_low(1)
            magic_numbers(2, down_nat, down_in)
            chunk_sums(0)
            other_taps(2, 3, b=0)
            time_steps(1)
            other_taps(4, b=0)
            fuse_up(0)
            other_taps(5, b=0)
            fuse_up(1)
            ffn_scales()
            other_taps(0, b=1)
            fuse_up(2)
            other_taps(1, b=1)
            for j in range(NP // 2):
                if j == NI:
                    ffn_result(0)
                if j:
                    fuse_up(j + 2)
                if j + 2 < NV:
                    other_taps(j + 2, b=1)
                if j == NM:
                    split_da(1)
                if j == NV:
                    x_times_dt(0)
                    masked_cb(0)
                if j == NV + 1:
                    spread_x(0)
            for n in range(NN):
                k = NP // 2 + 2 * n
                if n:
                    gated(n - 1)
                    mix_tile(n, 0)
                if n == 0:
                    ffn_result(1)
                next_state(2 * n)
                if n in (3, 6):
                    ffn_result(n // 3 + 1)
                if k + 2 < NP:
                    fuse_up(k + 2)
                if n == 0:
                    mix_tile(0, 0)
                    chunk_sums(1)
                    scale_inter(0)
                    mix_tile(0, 1)
                if n + 1 < NN:
                    x_times_dt(n + 1)
                    masked_cb(n + 1)
                if n:
                    mix_tile(n, 1)
                if n % NT < NT - 1:
                    next_state(2 * n + 1)
                if n:
                    mean_square(n - 1)
                if k + 3 < NP:
                    fuse_up(k + 3)
                if n:
                    scale_inter(n)
                    result(n - 1)
            gated(NN - 1)
            mean_square(NN - 1)
            result(NN - 1)


_INS = ['L0_attn_x', 'L0_attn_W_in', 'L0_attn_conv_w', 'L0_attn_conv_b', 'L0_attn_dt_bias', 'L0_attn_A_log',
        'L0_attn_D', 'L0_attn_norm_w', 'L0_attn_W_out', 'L0_ffn_gate_w', 'L0_ffn_up_w', 'L0_ffn_down_w',
        'L0_ffn_gate_scale', 'L0_ffn_up_scale', 'L0_ffn_down_scale']


def kernel(**inputs):
    import numpy as _np
    import concourse.bacc as _bacc
    from concourse import mybir as _mybir
    from concourse.bass_utils import run_bass_kernel_spmd as _run

    nc = _bacc.Bacc("TRN2", target_bir_lowering=False, num_devices=1)
    arrays, args = {}, []
    for name in _INS:
        a = _np.ascontiguousarray(inputs[name])
        arrays[f"in_{name}"] = a
        args.append(nc.dram_tensor(f"in_{name}", a.shape, _mybir.dt.from_np(a.dtype), kind="ExternalInput").ap())
    shape = inputs['L0_attn_x'].shape
    args.append(nc.dram_tensor("out_0", shape, _mybir.dt.float32, kind="ExternalOutput").ap())
    mamba_and_ffn_block(nc, *args)
    r = _run(nc, [arrays], core_ids=[0])
    return r.results[0]["out_0"]
```
